# Optimizing a Trainium2 kernel written in Bass

```python
import numpy as np
import jax
import jax.numpy as jnp

def _softmax(x, axis=-1):
    return jax.nn.softmax(x, axis=axis)

def _gelu(x):
    return jax.nn.gelu(x, approximate=True)

def _silu(x):
    return jax.nn.silu(x)

def _sigmoid(x):
    return jax.nn.sigmoid(x)

def _layernorm(x, axis=-1, eps=1e-05):
    m = jnp.mean(x, axis=axis, keepdims=True)
    v = jnp.var(x, axis=axis, keepdims=True)
    return (x - m) / jnp.sqrt(v + eps)

def _scatter_add(tgt, idx, src, axis=0):
    return tgt.at[idx].add(src)

def _segment_sum(src, seg, n):
    return jax.ops.segment_sum(src, seg, n)
kernel_name = 'mk_gnn_resnorm_d2_gnn_r32_443ba5'

def setup_inputs(seed: int=0):
    np.random.seed(seed)
    _w = jnp.asarray

    def _rec_inputs():
        import jax
        import jax.numpy as jnp
        _gk = jax.random.key(seed)
        x = -0.0006008 + 1.001 * jax.random.normal(jax.random.fold_in(_gk, 1), (3125, 128), jnp.float32)
        src = jax.random.randint(jax.random.fold_in(_gk, 2), (50000,), 0, 3125, jnp.int32)
        dst = jnp.minimum((3125 * jax.random.uniform(jax.random.fold_in(_gk, 3), (50000,)) ** 2.0).astype(jnp.int32), 99999)
        _o = jnp.argsort(dst, stable=True)
        src = src[_o]
        dst = dst[_o]
        edge_type_4 = jax.random.randint(jax.random.fold_in(_gk, 13), (50000,), 0, 4, jnp.int32)
        edge_weight = jax.random.uniform(jax.random.fold_in(_gk, 14), (50000,), jnp.float32, 0.0, 0.999996)
        return (x, src, dst, edge_type_4, edge_weight)
    x, src, dst, edge_type_4, edge_weight = _rec_inputs()

    def _L0_gnn_setup():
        import jax, jax.numpy as jnp
        import numpy as np
        NUM_RELATIONS = 4
        N_NODES = 625
        N_EDGES = 10000
        F_IN = 128
        HID = 128
        EMB = 128

        def _rgcn_conv(x, src, dst, edge_type, edge_weight, W, root, bias):
            xj = x[src]
            m = jnp.zeros((xj.shape[0], W.shape[2]), dtype=x.dtype)
            for r in range(W.shape[0]):
                mask = (edge_type == r).astype(x.dtype)[:, None]
                m = m + mask * (xj @ W[r])
            m = m * edge_weight[:, None]
            out = jax.ops.segment_sum(m, dst, num_segments=x.shape[0])
            return out + x @ root + bias
        key = jax.random.key(seed)
        ks = jax.random.split(key, 10)
        return {'x': jax.random.normal(ks[0], (N_NODES, F_IN), dtype=jnp.float32), 'edge_index': jax.random.randint(ks[1], (2, N_EDGES), 0, N_NODES, dtype=jnp.int64 if jax.config.jax_enable_x64 else jnp.int32).astype(jnp.int32), 'edge_type': jax.random.randint(ks[2], (N_EDGES,), 0, NUM_RELATIONS).astype(jnp.int32), 'edge_weight': jax.random.uniform(ks[3], (N_EDGES,), dtype=jnp.float32), 'W1': jax.random.normal(ks[4], (NUM_RELATIONS, F_IN, HID), dtype=jnp.float32) * 0.05, 'root1': jax.random.normal(ks[5], (F_IN, HID), dtype=jnp.float32) * 0.05, 'b1': jax.random.normal(ks[6], (HID,), dtype=jnp.float32) * 0.05, 'W2': jax.random.normal(ks[7], (NUM_RELATIONS, HID, EMB), dtype=jnp.float32) * 0.05, 'root2': jax.random.normal(ks[8], (HID, EMB), dtype=jnp.float32) * 0.05, 'b2': jax.random.normal(ks[9], (EMB,), dtype=jnp.float32) * 0.05}
    _L0_gnn_all = _L0_gnn_setup()
    _L0_gnn_in = {k: v for k, v in _L0_gnn_all.items() if k in ('W1', 'root1', 'b1', 'W2', 'root2', 'b2')}
    del _L0_gnn_all

    def _L1_gnn_setup():
        import jax, jax.numpy as jnp
        import numpy as np
        N_NODES = 50000
        N_EDGES = 20000
        H_DIM = 128
        key = jax.random.key(seed)
        k1, k2, k3, k4 = jax.random.split(key, 4)
        node_feat = jax.random.normal(k1, (N_NODES, H_DIM), dtype=jnp.float32)
        src = jax.random.randint(k2, (N_EDGES,), 0, N_NODES, dtype=jnp.int64)
        dst = jax.random.randint(k3, (N_EDGES,), 0, N_NODES, dtype=jnp.int64)
        limit = np.sqrt(6.0 / (2 * H_DIM + H_DIM)).astype(np.float32)
        W = jax.random.uniform(k4, (2 * H_DIM, H_DIM), minval=-limit, maxval=limit, dtype=jnp.float32)
        b = jnp.zeros((H_DIM,), dtype=jnp.float32)
        return {'node_feat': node_feat, 'src': src, 'dst': dst, 'W': W, 'b': b}
    _L1_gnn_all = _L1_gnn_setup()
    _L1_gnn_in = {k: v for k, v in _L1_gnn_all.items() if k in ('W', 'b')}
    del _L1_gnn_all
    return {'x': x, 'src': src, 'dst': dst, 'edge_type_4': edge_type_4, 'edge_weight': edge_weight, 'L0_gnn_W1': _L0_gnn_in['W1'], 'L0_gnn_root1': _L0_gnn_in['root1'], 'L0_gnn_b1': _L0_gnn_in['b1'], 'L0_gnn_W2': _L0_gnn_in['W2'], 'L0_gnn_root2': _L0_gnn_in['root2'], 'L0_gnn_b2': _L0_gnn_in['b2'], 'L1_gnn_W': _L1_gnn_in['W'], 'L1_gnn_b': _L1_gnn_in['b']}

def reference(x, src, dst, edge_type_4, edge_weight, L0_gnn_W1, L0_gnn_root1, L0_gnn_b1, L0_gnn_W2, L0_gnn_root2, L0_gnn_b2, L1_gnn_W, L1_gnn_b):
    import jax
    import jax.numpy as jnp

    def _L0_gnn_ref(x, edge_index, edge_type, edge_weight, W1, root1, b1, W2, root2, b2):
        import jax, jax.numpy as jnp
        import numpy as np
        NUM_RELATIONS = 4
        N_NODES = 625
        N_EDGES = 10000
        F_IN = 128
        HID = 128
        EMB = 128

        def _rgcn_conv(x, src, dst, edge_type, edge_weight, W, root, bias):
            xj = x[src]
            m = jnp.zeros((xj.shape[0], W.shape[2]), dtype=x.dtype)
            for r in range(W.shape[0]):
                mask = (edge_type == r).astype(x.dtype)[:, None]
                m = m + mask * (xj @ W[r])
            m = m * edge_weight[:, None]
            out = jax.ops.segment_sum(m, dst, num_segments=x.shape[0])
            return out + x @ root + bias
        src, dst = (edge_index[0], edge_index[1])
        ew = (edge_weight - edge_weight.min()) / (edge_weight.max() - edge_weight.min() + 1e-08)
        h = jax.nn.relu(_rgcn_conv(x, src, dst, edge_type, ew, W1, root1, b1))
        h = _rgcn_conv(h, src, dst, edge_type, ew, W2, root2, b2)
        return h

    def _L1_gnn_ref(node_feat, src, dst, W, b):
        import jax, jax.numpy as jnp
        import numpy as np
        N_NODES = 50000
        N_EDGES = 20000
        H_DIM = 128
        msg = jnp.concatenate([node_feat[src], node_feat[dst]], axis=-1)
        edge_feat = msg @ W + b
        agg = jax.ops.segment_sum(edge_feat, dst, num_segments=node_feat.shape[0])
        return jax.nn.sigmoid(agg) + jax.nn.softplus(node_feat)
    edge_index = jnp.stack([src, dst])
    x = _layernorm(x + _L0_gnn_ref(x, edge_index, edge_type_4, edge_weight, L0_gnn_W1, L0_gnn_root1, L0_gnn_b1, L0_gnn_W2, L0_gnn_root2, L0_gnn_b2), axis=-1)
    x = _layernorm(x + _L1_gnn_ref(x, src, dst, L1_gnn_W, L1_gnn_b), axis=-1)
    return x

_drawn_inputs = setup_inputs


def setup_inputs(seed=0):
    import zlib

    import numpy as np

    out = dict(_drawn_inputs(seed))
    spreads = {'L1_gnn_b': (0.0, 0.1)}
    factors = {}
    for name, (base, spread) in spreads.items():
        noise = np.random.default_rng([zlib.crc32(name.encode()), seed]).standard_normal(out[name].shape)
        drawn = base * np.exp(spread * noise) if base else spread * noise
        out[name] = jnp.asarray(drawn.astype(out[name].dtype))
    for name, factor in factors.items():
        out[name] = (out[name] * factor).astype(out[name].dtype)
    return out
```

```python
import numpy as np
import concourse.bass as bass
from concourse import mybir
from contextlib import ExitStack

N_NODES, FEAT, N_EDGES, RELS = 3125, 128, 50000, 4
P = 128
BLOCKS = -(-N_NODES // P)
NP = BLOCKS * P
TILES = -(-N_EDGES // P)
LAST_EDGES = N_EDGES - (TILES - 1) * P
U = 17
ITERS = TILES // U
HALVES = [(0, 9), (9, U)]
assert ITERS * U == TILES
BANK = 512
WIN = 64
STRIDE = BANK - WIN
BANKS = -(-N_NODES // STRIDE)
DEG = BANKS * BANK
ALLN = BANKS * STRIDE
GROUPS = -(-BLOCKS // 4)
STAGES = 4
EPS = 1e-5


def group_blocks(g):
    return min(4, BLOCKS - 4 * g)


def build(nc, x, srcs, dsts, types, weights, w1, root1, b1, w2, root2, b2, w3, b3, out):
    fp32, bf16, i32 = mybir.dt.float32, mybir.dt.bfloat16, mybir.dt.int32
    ALU, ACT, AX = mybir.AluOpType, mybir.ActivationFunctionType, mybir.AxisListType

    tables = [nc.dram_tensor(f"table{n}", (NP, RELS * FEAT if n < 2 else FEAT), fp32, kind="Internal").ap()
              for n in range(3)]
    rows = [t.rearrange("n (r f) -> (n r) f", f=FEAT) for t in tables[:2]] + [tables[2]]

    with ExitStack() as ctx:
        def sb(name, shape, dt=fp32):
            return ctx.enter_context(nc.sbuf_tensor(name, shape, dt))

        def sem(name):
            return ctx.enter_context(nc.semaphore(name))

        x_nm = sb("x_nm", [P, BLOCKS, FEAT])
        src_i = sb("src_i", [P, TILES], i32)
        dst_i = sb("dst_i", [P, TILES], i32)
        typ_i = sb("typ_i", [P, TILES], i32)
        ew = sb("ew", [P, TILES])
        wall = [sb(f"wall{n}", [P, RELS, FEAT]) for n in range(2)]
        root = [sb(f"root{n}", [P, FEAT]) for n in range(2)]
        bias = [sb(f"bias{n}", [P, 1]) for n in range(2)]
        wtop = sb("wtop", [P, FEAT])
        wbot = sb("wbot", [P, FEAT])
        b3row = sb("b3row", [8, FEAT])
        iota = sb("iota", [P, ALLN])
        part = sb("part", [P, 1])
        ident = sb("ident", [P, P])
        ones_row = sb("ones_row", [1, P])
        zeros = sb("zeros", [P, BANK], bf16)
        row_sel = sb("row_sel", [8, BANKS, P])
        bank_col = sb("bank_col", [P, BANKS, 8], bf16)
        eps = sb("eps", [P, 1])
        dst_f = sb("dst_f", [P, TILES])
        base_f = sb("base_f", [P, TILES])
        rel_f = sb("rel_f", [P, TILES])
        bank_f = sb("bank_f", [P, TILES])
        idx12 = sb("idx12", [P, TILES], i32)
        w12 = sb("w12", [P, TILES])
        w3m = sb("w3m", [P, TILES])
        col_i = sb("col_i", [1, TILES], i32)
        deg_col_i = sb("deg_col_i", [1, TILES], i32)
        col_t = sb("col_t", [1, TILES])
        ext = sb("ext", [P, 4])
        ext_all = sb("ext_all", [P, 4])
        scale2 = sb("scale2", [P, 2])
        ok_f = sb("ok_f", [1, 2])
        ok_i = sb("ok_i", [1, 1], i32)
        idx_slot = sb("idx_slot", [P, U], i32)
        msg = sb("msg", [P, U, FEAT])
        sel = sb("sel", [P, U, WIN])
        deg_sel = sb("deg_sel", [P, U, WIN], bf16)
        deg_bank = sb("deg_bank", [P, U, 8], bf16)
        wide_sel = sb("wide_sel", [P, 2, ALLN])
        wide_deg = sb("wide_deg", [P, 2, ALLN], bf16)
        stage = sb("stage", [P, STAGES, BANK])
        x_t = sb("x_t", [P, NP])
        h_t = sb("h_t", [P, NP])
        z_t = sb("z_t", [P, NP])
        x2_nm = sb("x2_nm", [P, BLOCKS, FEAT])
        x2_t = sb("x2_t", [P, NP])
        u_nm = x_nm
        deg_sb = sb("deg_sb", [8, BANK])
        b3_sel = sb("b3_sel", [8, BANKS, FEAT])
        deg_x = sb("deg_x", [P, BANKS, BANK])
        shared = sb("shared", [P, BANKS - 1, WIN])
        shared2 = sb("shared2", [P, BANKS - 1, WIN])
        stats = sb("stats", [P, BLOCKS, 6])
        mv = sb("mv", [P, BLOCKS, 2])
        rstd = sb("rstd", [P, BLOCKS])
        nmr = sb("nmr", [P, BLOCKS])

        ps = ctx.enter_context(nc.psum_tensor("ps", [P, 8 * BANK], fp32))
        acc = ps[:, 0:BANKS * BANK].rearrange("p (j c) -> p j c", c=BANK)

        def tail_of(t):
            return t[:, 0:ALLN].rearrange("p (j c) -> p j c", c=STRIDE)[:, 1:BANKS, 0:WIN]

        s_ld_x, s_ld_e, s_ld_w = sem("s_ld_x"), sem("s_ld_e"), sem("s_ld_w")
        s_clear, s_const, s_order = sem("s_clear"), sem("s_const"), sem("s_order")
        s_dstf, s_base_mm, s_ext, s_ext_all, s_edges = (
            sem("s_dstf"), sem("s_base_mm"), sem("s_ext"), sem("s_ext_all"), sem("s_edges"))
        s_xt_mm, s_xt = sem("s_xt_mm"), sem("s_xt")
        s_tab_mm, s_tab_sb = sem("s_tab_mm"), sem("s_tab_sb")
        s_tab_out = [sem(f"s_tab_out{n}") for n in range(STAGES)]
        s_idx, s_gate = sem("s_idx"), sem("s_gate")
        s_msg = [sem(f"s_msg{k}") for k in range(U)]
        s_sel, s_deg_sel, s_used = sem("s_sel"), sem("s_deg_sel"), sem("s_used")
        s_sum, s_deg_sum = sem("s_sum"), sem("s_deg_sum")
        s_deg, s_b3, s_deg_mm, s_deg_b = sem("s_deg"), sem("s_b3"), sem("s_deg_mm"), sem("s_deg_b")
        s_h_act, s_h_dve = sem("s_h_act"), sem("s_h_dve")
        s_z, s_zn, s_stat, s_std, s_rstd, s_x2 = (
            sem("s_z"), sem("s_zn"), sem("s_stat"), sem("s_std"), sem("s_rstd"), sem("s_x2"))
        s_x2t_mm, s_x2t, s_dx, s_sp, s_u = sem("s_x2t_mm"), sem("s_x2t"), sem("s_dx"), sem("s_sp"), sem("s_u")
        s_ov, s_sig, s_sn, s_stat2, s_std2, s_rstd2, s_y, s_out = (
            sem("s_ov"), sem("s_sig"), sem("s_sn"), sem("s_stat2"), sem("s_std2"), sem("s_rstd2"),
            sem("s_y"), sem("s_out"))
        block = ctx.enter_context(nc.Block())

        FIRST_PIECE = [0, BLOCKS, 2 * BLOCKS, 2 * BLOCKS + GROUPS]
        BATCHES = [(0, 16), (16, BLOCKS)]

        def batch_of(b):
            return next(n for n, (lo, hi) in enumerate(BATCHES) if lo <= b < hi)

        def table_done(layer, slot):
            return 16 * len([n for n in range(FIRST_PIECE[layer + 1]) if n % STAGES == slot])

        @block.sync
        def _(sp):
            sp.dma_start(dst_i[:, :], dsts).then_inc(s_ld_e, 16)
            sp.dma_start(x_nm[:, :, :], x.rearrange("(b p) f -> p b f", p=P)).then_inc(s_ld_x, 16)
            sp.dma_start(wall[0][:, :, :], w1.rearrange("r i o -> i r o")).then_inc(s_ld_w, 16)
            sp.dma_start(root[0][:, :], root1).then_inc(s_ld_w, 16)
            sp.dma_start(bias[0][:, :], b1.rearrange("(f a) -> f a", a=1)).then_inc(s_ld_w, 16)
            sp.dma_start(wall[1][:, :, :], w2.rearrange("r i o -> i r o")).then_inc(s_ld_w, 16)
            sp.dma_start(root[1][:, :], root2).then_inc(s_ld_w, 16)
            sp.dma_start(bias[1][:, :], b2.rearrange("(f a) -> f a", a=1)).then_inc(s_ld_w, 16)
            sp.dma_start(wtop[:, :], w3[0:FEAT, :]).then_inc(s_ld_w, 16)
            sp.dma_start(wbot[:, :], w3[FEAT:2 * FEAT, :]).then_inc(s_ld_w, 16)
            sp.dma_start(b3row[:, :], b3.rearrange("(a f) -> a f", a=1).to_broadcast([8, FEAT])).then_inc(s_ld_w, 16)
            for layer in range(3):
                for n in range(FIRST_PIECE[layer], FIRST_PIECE[layer + 1]):
                    sp.wait_ge(s_tab_sb, n + 1)
                    b = n - FIRST_PIECE[layer]
                    if layer < 2:
                        dest, piece = tables[layer][b * P:(b + 1) * P, :], stage[:, n % STAGES, :]
                    else:
                        k = group_blocks(b)
                        dest = tables[2][4 * b * P:(4 * b + k) * P, :].rearrange("(q p) f -> p q f", p=P)
                        piece = stage[:, n % STAGES, 0:k * FEAT].rearrange("p (q f) -> p q f", f=FEAT)
                    sp.dma_start(dest, piece).then_inc(s_tab_out[n % STAGES], 16)
            count = 0
            for g in range(GROUPS):
                sp.wait_ge(s_y, min(4 * g + 4, BLOCKS))
                full = [b for b in range(4 * g, 4 * g + group_blocks(g)) if (b + 1) * P <= N_NODES]
                if full:
                    lo, hi = full[0], full[-1] + 1
                    sp.dma_start(out[lo * P:hi * P, :].rearrange("(b p) f -> p b f", p=P),
                                 x2_nm[:, lo:hi, :]).then_inc(s_out, 16)
                    count += 1
                if len(full) < group_blocks(g):
                    sp.dma_start(out[(BLOCKS - 1) * P:N_NODES, :],
                                 x2_nm[0:N_NODES - (BLOCKS - 1) * P, BLOCKS - 1, :]).then_inc(s_out, 16)
                    count += 1
            sp.wait_ge(s_out, 16 * count)

        @block.gpsimd
        def _(pool):
            nc.gpsimd.memset(ident[:, :], 0.0).then_inc(s_clear, 1)
            nc.gpsimd.memset(row_sel[:, :, :], 0.0).then_inc(s_clear, 1)
            nc.gpsimd.iota(iota[:, :], [[1, ALLN]], base=0, channel_multiplier=0,
                           allow_small_or_imprecise_dtypes=True).then_inc(s_const, 1)
            nc.gpsimd.iota(part[:, :], [[0, 1]], base=0, channel_multiplier=1,
                           allow_small_or_imprecise_dtypes=True).then_inc(s_const, 1)
            pool.wait_ge(s_clear, 2)
            nc.gpsimd.affine_select(out=ident[:, :], in_=ident[:, :], compare_op=ALU.not_equal, fill=1.0,
                                    base=0, pattern=[[-1, P]], channel_multiplier=1).then_inc(s_const, 1)
            nc.gpsimd.affine_select(out=row_sel[:, :, :], in_=row_sel[:, :, :], compare_op=ALU.not_equal,
                                    fill=1.0, base=0, pattern=[[-1, BANKS], [0, P]],
                                    channel_multiplier=1).then_inc(s_const, 1)
            pool.wait_ge(s_ext, 4)
            nc.gpsimd.partition_all_reduce(ext_all[:, :], ext[:, :], P, bass.bass_isa.ReduceOp.max)\
                .then_inc(s_ext_all, 1)
            for layer in range(3):
                for n in range(STAGES):
                    pool.wait_ge(s_tab_out[n], table_done(layer, n))
                with pool.Fori(0, ITERS) as i:
                    for half, (lo, hi) in enumerate(HALVES):
                        pool.wait_ge(s_idx, 2 * i + (2 * ITERS * layer + half + 1))
                        pool.sem_inc(s_gate, 1)
                        for k in range(lo, hi):
                            pool.indirect_dma_start(
                                msg[:, k, :], None, rows[layer],
                                bass.IndirectOffsetOnAxis(idx_slot[:, k:k + 1], 0)).then_inc(s_msg[k], 16)

        @block.scalar
        def _(act):
            act.dma_start(src_i[:, :], srcs).then_inc(s_ld_e, 16)
            act.dma_start(typ_i[:, :], types).then_inc(s_ld_e, 16)
            act.dma_start(ew[:, :], weights).then_inc(s_ld_e, 16)

            def table_pieces(layer):
                for n in range(FIRST_PIECE[layer], FIRST_PIECE[layer + 1]):
                    act.wait_ge(s_tab_mm, n + 1)
                    if n >= STAGES:
                        act.wait_ge(s_tab_out[n % STAGES], 16 * (n // STAGES))
                    width = BANK if layer < 2 else group_blocks(n - FIRST_PIECE[layer]) * FEAT
                    bank = BANKS if n % 2 == 0 else 0
                    nc.scalar.copy(stage[:, n % STAGES, 0:width], ps[:, bank * BANK:bank * BANK + width])\
                        .then_inc(s_tab_sb, 1)

            def indices(layer, lo_iter, hi_iter):
                table = idx12 if layer < 2 else src_i
                with act.Fori(lo_iter, hi_iter) as i:
                    for lo, hi in HALVES:
                        act.wait_ge(s_used, U * i + (U * ITERS * layer + hi))
                        nc.scalar.copy(idx_slot[:, lo:hi], table[:, bass.ds(U * i + lo, hi - lo)])\
                            .then_inc(s_idx, 1)

            for g in range(GROUPS):
                act.wait_ge(s_xt_mm, g + 1)
                w = group_blocks(g) * P
                nc.scalar.copy(x_t[:, g * BANK:g * BANK + w], ps[:, g * BANK:g * BANK + w]).then_inc(s_xt, 1)
            table_pieces(0)
            act.wait_ge(s_edges, 1)
            indices(0, 0, ITERS)
            act.wait_ge(s_h_dve, 1)
            for j in range(BANKS):
                lo = 0 if j == 0 else WIN
                nc.scalar.activation(h_t[:, j * STRIDE + lo:(j + 1) * STRIDE], acc[:, j, lo:STRIDE],
                                     ACT.Relu, bias=bias[0][:, 0:1]).then_inc(s_h_act, 1)
            table_pieces(1)
            for j in range(BANKS):
                act.wait_ge(s_deg_mm, j + 1)
                nc.scalar.copy(deg_x[:, j, :], acc[:, j, :]).then_inc(s_deg_b, 1)
            indices(1, 0, ITERS)
            for n, (lo, hi) in enumerate(BATCHES):
                act.wait_ge(s_stat, n + 1)
                nc.scalar.activation(rstd[:, lo:hi], mv[:, lo:hi, 1], ACT.Sqrt, bias=eps[:, 0:1]).then_inc(s_std, 1)
                act.wait_ge(s_rstd, n + 1)
                for b in range(lo, hi):
                    nc.scalar.activation(x2_nm[:, b, :], ps[:, b * P:(b + 1) * P], ACT.Identity,
                                         bias=nmr[:, b:b + 1], scale=rstd[:, b:b + 1]).then_inc(s_x2, 1)
            table_pieces(2)
            indices(2, 0, 2)
            act.wait_ge(s_x2, BLOCKS)
            nc.scalar.activation(u_nm[:, :, :], x2_nm[:, :, :], ACT.Exp).then_inc(s_sp, 1)
            act.wait_ge(s_sp, 1)
            nc.scalar.activation(u_nm[:, :, :], u_nm[:, :, :], ACT.Ln, bias=1.0).then_inc(s_sp, 1)
            indices(2, 2, ITERS)
            act.wait_ge(s_ov, 1)
            for j in range(BANKS):
                lo = 0 if j == 0 else WIN
                nc.scalar.activation(z_t[:, j * STRIDE + lo:(j + 1) * STRIDE], acc[:, j, lo:STRIDE],
                                     ACT.Sigmoid).then_inc(s_sig, 1)
            nc.scalar.activation(tail_of(z_t), shared2[:, :, :], ACT.Sigmoid).then_inc(s_sig, 1)
            for n, (lo, hi) in enumerate(BATCHES):
                act.wait_ge(s_stat2, n + 1)
                nc.scalar.activation(rstd[:, lo:hi], mv[:, lo:hi, 1], ACT.Sqrt, bias=eps[:, 0:1]).then_inc(s_std2, 1)
                act.wait_ge(s_rstd2, n + 1)
                for b in range(lo, hi):
                    nc.scalar.activation(x2_nm[:, b, :], u_nm[:, b, :], ACT.Identity,
                                         bias=nmr[:, b:b + 1], scale=rstd[:, b:b + 1]).then_inc(s_y, 1)

        @block.vector
        def _(dve):
            chain = [0]

            def link(ins):
                chain[0] += 1
                ins.then_inc(s_order, 1)
                dve.wait_ge(s_order, chain[0])

            V = nc.vector
            V.memset(ones_row[:, :], 1.0).then_inc(s_const, 1)
            V.memset(zeros[:, :], 0.0).then_inc(s_const, 1)
            V.memset(eps[:, :], EPS).then_inc(s_const, 1)
            link(V.memset(bank_col[:, :, :], 0.0))
            V.memset(bank_col[:, :, :].rearrange("p a b -> p (a b)")[:, 0:8 * BANKS:9], 1.0).then_inc(s_const, 1)
            V.memset(h_t[:, ALLN:NP], 0.0).then_inc(s_const, 1)
            V.memset(z_t[:, ALLN:NP], 0.0).then_inc(s_const, 1)
            V.memset(w3m[:, :], 1.0).then_inc(s_const, 1)
            dve.wait_ge(s_ld_e, 64)
            V.tensor_copy(dst_f[:, :], dst_i[:, :]).then_inc(s_dstf, 1)
            link(V.scalar_tensor_tensor(idx12[:, :], src_i[:, :], float(RELS), typ_i[:, :], ALU.mult, ALU.add))
            V.reduce_max(ext[:, 0:1], ew[:, :], axis=AX.X).then_inc(s_ext, 1)
            V.tensor_reduce(ext[:, 1:2], ew[:, :], AX.X, ALU.min, negate=True).then_inc(s_ext, 1)
            dve.wait_ge(s_base_mm, 1)
            link(V.tensor_copy(base_f[:, :], ps[:, DEG:DEG + TILES]))
            link(V.tensor_tensor(rel_f[:, :], dst_f[:, :], base_f[:, :], ALU.subtract))
            V.reduce_max(ext[:, 2:3], rel_f[:, :], axis=AX.X).then_inc(s_ext, 1)
            V.tensor_reduce(ext[:, 3:4], rel_f[:, :], AX.X, ALU.min, negate=True).then_inc(s_ext, 1)
            link(V.tensor_single_scalar(bank_f[:, :], base_f[:, :], float(STRIDE), ALU.is_ge))
            for j in range(2, BANKS):
                link(V.scalar_tensor_tensor(bank_f[:, :], base_f[:, :], float(STRIDE * j), bank_f[:, :],
                                            ALU.is_ge, ALU.add))
            V.scalar_tensor_tensor(col_i[:, :], bank_f[0:1, :], float(WIN), base_f[0:1, :], ALU.mult, ALU.add)\
                .then_inc(s_edges, 1)
            link(V.scalar_tensor_tensor(col_t[:, :], bank_f[0:1, :], -float(STRIDE), base_f[0:1, :],
                                        ALU.mult, ALU.add))
            V.tensor_scalar_add(deg_col_i[:, :], col_t[:, :], float(DEG)).then_inc(s_edges, 1)
            dve.wait_ge(s_const, 11)
            link(V.tensor_single_scalar(w3m[:, TILES - 1:TILES], part[:, :], float(LAST_EDGES), ALU.is_lt))
            dve.wait_ge(s_ext_all, 1)
            link(V.tensor_tensor(scale2[:, 0:1], ext_all[:, 0:1], ext_all[:, 1:2], ALU.add))
            link(V.tensor_scalar_add(scale2[:, 0:1], scale2[:, 0:1], 1e-8))
            link(V.reciprocal(scale2[:, 1:2], scale2[:, 0:1]))
            link(V.tensor_scalar(w12[:, :], ew[:, :], ext_all[:, 1:2], scale2[:, 1:2], ALU.add, ALU.mult))
            link(V.tensor_tensor(w12[:, TILES - 1:TILES], w12[:, TILES - 1:TILES], w3m[:, TILES - 1:TILES],
                                 ALU.mult))
            link(V.tensor_single_scalar(ok_f[:, 0:1], ext_all[0:1, 2:3], float(WIN), ALU.is_lt))
            link(V.tensor_single_scalar(ok_f[:, 1:2], ext_all[0:1, 3:4], 0.0, ALU.is_le))
            link(V.tensor_tensor(ok_i[:, :], ok_f[:, 0:1], ok_f[:, 1:2], ALU.mult))
            dve.wait_ge(s_ld_w, 144)
            V.tensor_tensor(b3_sel[:, :, :], row_sel[:, :, :],
                            b3row[:, :].unsqueeze(1).to_broadcast([8, BANKS, FEAT]), ALU.mult).then_inc(s_b3, 1)
            V.engine_nop().then_inc(s_edges, 1)
            sorted_flag = dve.value_load(ok_i[0:1, 0:1], min_val=0, max_val=1)

            def selections(layer):
                w = w12 if layer < 2 else w3m
                tiles_before = U * ITERS * layer
                with dve.If(sorted_flag == 1):
                    with dve.Fori(0, ITERS) as i:
                        for lo, hi in HALVES:
                            dve.wait_ge(s_used, U * i + (tiles_before + hi))
                            for k in range(lo, hi):
                                rel = rel_f[:, bass.ds(U * i + k, 1)]
                                V.tensor_scalar(sel[:, k, :], iota[:, 0:WIN], rel, w[:, bass.ds(U * i + k, 1)],
                                                ALU.is_equal, ALU.mult).then_inc(s_sel, 1)
                                if layer == 0:
                                    V.tensor_scalar(deg_sel[:, k, :], iota[:, 0:WIN], rel,
                                                    w3m[:, bass.ds(U * i + k, 1)],
                                                    ALU.is_equal, ALU.mult).then_inc(s_deg_sel, 1)
                                    V.tensor_scalar(deg_bank[:, k, :], iota[:, 0:8],
                                                    bank_f[:, bass.ds(U * i + k, 1)], None,
                                                    ALU.is_equal).then_inc(s_deg_sel, 1)
                with dve.Else():
                    with dve.Fori(0, ITERS) as i:
                        for k in range(U):
                            done = k if k == 0 else k - 1
                            dve.wait_ge(s_used, U * i + (tiles_before + U + done))
                            dst = dst_f[:, bass.ds(U * i + k, 1)]
                            V.tensor_scalar(wide_sel[:, k % 2, :], iota[:, :], dst, w[:, bass.ds(U * i + k, 1)],
                                            ALU.is_equal, ALU.mult).then_inc(s_sel, 1)
                            if layer == 0:
                                V.tensor_scalar(wide_deg[:, k % 2, :], iota[:, :], dst,
                                                w3m[:, bass.ds(U * i + k, 1)],
                                                ALU.is_equal, ALU.mult).then_inc(s_deg_sel, 2)

            selections(0)
            dve.wait_ge(s_sum, BANKS)
            link(V.tensor_scalar(shared[:, :, :], acc[:, 0:BANKS - 1, STRIDE:BANK], bias[0][:, 0:1], None, ALU.add))
            V.tensor_tensor(shared2[:, :, :], acc[:, 1:BANKS, 0:WIN], shared[:, :, :], ALU.add).then_inc(s_h_dve, 1)
            dve.wait_ge(s_h_dve, 1)
            V.tensor_scalar(tail_of(h_t), shared2[:, :, :], 0.0, None, ALU.max).then_inc(s_h_dve, 1)
            dve.wait_ge(s_deg_sum, 1)
            V.tensor_copy(deg_sb[:, :], ps[0:8, DEG:DEG + BANK]).then_inc(s_deg, 1)

            selections(1)
            for j in range(BANKS):
                dve.wait_ge(s_sum, BANKS + j + 1)
                c = slice(j * STRIDE, (j + 1) * STRIDE)
                link(V.scalar_tensor_tensor(z_t[:, c], acc[:, j, 0:STRIDE], bias[1][:, 0:1], x_t[:, c],
                                            ALU.add, ALU.add))
            V.tensor_tensor(tail_of(z_t), acc[:, 0:BANKS - 1, STRIDE:BANK], tail_of(z_t), ALU.add).then_inc(s_z, 1)
            for n, (lo, hi) in enumerate(BATCHES):
                for b in range(lo, hi):
                    if b % 4 == 0:
                        dve.wait_ge(s_zn, b // 4 + 1)
                    last = V.bn_stats(stats[:, b, :], ps[:, b * P:(b + 1) * P])
                    if b < hi - 1:
                        last.then_inc(s_order, 1)
                        chain[0] += 1
                link(last)
                for b in range(lo, hi):
                    last = V.bn_aggr(mv[:, b, :], stats[:, b, :])
                    if b < hi - 1:
                        last.then_inc(s_order, 1)
                        chain[0] += 1
                last.then_inc(s_stat, 1)
            for n, (lo, hi) in enumerate(BATCHES):
                dve.wait_ge(s_std, n + 1)
                link(V.reciprocal(rstd[:, lo:hi], rstd[:, lo:hi]))
                V.scalar_tensor_tensor(nmr[:, lo:hi], mv[:, lo:hi, 0], -1.0, rstd[:, lo:hi],
                                       ALU.mult, ALU.mult).then_inc(s_rstd, 1)
            for g in range(GROUPS):
                dve.wait_ge(s_x2t_mm, g + 1)
                w = group_blocks(g) * P
                V.tensor_copy(x2_t[:, g * BANK:g * BANK + w], ps[:, g * BANK:g * BANK + w]).then_inc(s_x2t, 1)
            dve.wait_ge(s_deg_b, BANKS)
            dve.wait_ge(s_x2t, GROUPS)
            for j in range(BANKS):
                V.tensor_tensor(deg_x[:, j, :], deg_x[:, j, :], x2_t[:, j * STRIDE:j * STRIDE + BANK],
                                ALU.mult).then_inc(s_dx, 1)
            dve.wait_ge(s_x2, BLOCKS)

            selections(2)
            dve.wait_ge(s_sp, 2)
            link(V.tensor_tensor(u_nm[:, :, :], u_nm[:, :, :], x2_nm[:, :, :], ALU.add))
            dve.wait_ge(s_sum, 3 * BANKS)
            link(V.tensor_copy(shared[:, :, :], acc[:, 0:BANKS - 1, STRIDE:BANK]))
            V.tensor_tensor(shared2[:, :, :], acc[:, 1:BANKS, 0:WIN], shared[:, :, :], ALU.add).then_inc(s_ov, 1)
            for n, (lo, hi) in enumerate(BATCHES):
                for b in range(lo, hi):
                    if b % 4 == 0:
                        dve.wait_ge(s_sn, b // 4 + 1)
                        e = b + group_blocks(b // 4)
                        link(V.tensor_tensor(u_nm[:, b:e, :], ps[:, b * P:e * P].rearrange("p (b f) -> p b f", f=P),
                                             u_nm[:, b:e, :], ALU.add))
                    last = V.bn_stats(stats[:, b, :], u_nm[:, b, :])
                    if b < hi - 1:
                        last.then_inc(s_order, 1)
                        chain[0] += 1
                link(last)
                for b in range(lo, hi):
                    last = V.bn_aggr(mv[:, b, :], stats[:, b, :])
                    if b < hi - 1:
                        last.then_inc(s_order, 1)
                        chain[0] += 1
                last.then_inc(s_stat2, 1)
            for n, (lo, hi) in enumerate(BATCHES):
                dve.wait_ge(s_std2, n + 1)
                link(V.reciprocal(rstd[:, lo:hi], rstd[:, lo:hi]))
                V.scalar_tensor_tensor(nmr[:, lo:hi], mv[:, lo:hi, 0], -1.0, rstd[:, lo:hi],
                                       ALU.mult, ALU.mult).then_inc(s_rstd2, 1)

        @block.tensor
        def _(pe):
            T = nc.tensor

            def table(layer, source, weight, ready=lambda b: None):
                for n in range(FIRST_PIECE[layer], FIRST_PIECE[layer + 1]):
                    if n >= 2:
                        pe.wait_ge(s_tab_sb, n - 1)
                    bank = BANKS if n % 2 == 0 else 0
                    b = n - FIRST_PIECE[layer]
                    ready(b)
                    if layer < 2:
                        last = T.matmul(ps[:, bank * BANK:(bank + 1) * BANK], source[:, b * P:(b + 1) * P],
                                        weight, start=True, stop=True)
                    else:
                        for q in range(group_blocks(b)):
                            c = bank * BANK + q * FEAT
                            last = T.matmul(ps[:, c:c + FEAT], source[:, (4 * b + q) * P:(4 * b + q + 1) * P],
                                            weight, start=True, stop=True)
                    last.then_inc(s_tab_mm, 1)

            def clear(j, rows=P):
                T.matmul(ps[0:rows, j * BANK:(j + 1) * BANK], zeros[:, 0:rows], zeros[:, :], start=True, stop=False,
                         skip_group_check=True)

            def close(j, rows=P):
                return T.matmul(ps[0:rows, j * BANK:(j + 1) * BANK], zeros[:, 0:rows], zeros[:, :], start=False,
                                stop=True, skip_group_check=True)

            def transposes(source, done, ready=None):
                for g in range(GROUPS):
                    for b in range(4 * g, 4 * g + group_blocks(g)):
                        if ready:
                            ready(b)
                        last = T.transpose(ps[:, b * P:(b + 1) * P], source(b), ident[:, :])
                    last.then_inc(done, 1)

            pe.sem_inc(s_used, U)
            pe.wait_ge(s_const, 11)
            pe.wait_ge(s_dstf, 1)
            T.matmul(ps[:, DEG:DEG + TILES], ones_row[:, :], dst_f[0:1, :], start=True, stop=True)\
                .then_inc(s_base_mm, 1)
            pe.wait_ge(s_ld_x, 16)
            transposes(lambda b: x_nm[:, b, :], s_xt_mm)
            pe.wait_ge(s_ld_w, 144)
            pe.wait_ge(s_edges, 2)
            table(0, x_t, wall[0][:, :, :].rearrange("p r f -> p (r f)"),
                  lambda b: pe.wait_ge(s_xt, b // 4 + 1))
            pe.wait_ge(s_edges, 3)
            sorted_flag = pe.value_load(ok_i[0:1, 0:1], min_val=0, max_val=1)

            def registers(values, least, most):
                return nc.values_load_multi_w_load_instructions(
                    values, engines=[mybir.EngineType.PE], min_val=least, max_val=most,
                    skip_runtime_bounds_check_because="worked out from destinations, which are nodes")[1]

            def sums(layer):
                tiles_before = U * ITERS * layer
                with pe.If(sorted_flag == 1):
                    with pe.Fori(0, ITERS) as i:
                        for lo, hi in HALVES:
                            cols = registers(col_i[0:1, bass.ds(U * i + lo, hi - lo)], 0, BANKS * BANK - WIN)
                            if layer == 0:
                                deg_cols = registers(deg_col_i[0:1, bass.ds(U * i + lo, hi - lo)],
                                                     DEG, 8 * BANK - WIN)
                            for k in range(lo, hi):
                                pe.wait_ge(s_msg[k], 16 * i + 16 * (ITERS * layer + 1))
                                pe.wait_ge(s_sel, U * i + (tiles_before + k + 1))
                                last = T.matmul(ps[:, bass.ds(cols[k - lo], WIN)], msg[:, k, :], sel[:, k, :],
                                                start=False, stop=False, skip_group_check=True)
                                if layer == 0:
                                    pe.wait_ge(s_deg_sel, 2 * U * i + 2 * (k + 1))
                                    last = T.matmul(ps[0:8, bass.ds(deg_cols[k - lo], WIN)], deg_bank[:, k, :],
                                                    deg_sel[:, k, :], start=False, stop=False,
                                                    skip_group_check=True)
                                last.then_inc(s_used, 1)
                with pe.Else():
                    with pe.Fori(0, ITERS) as i:
                        for k in range(U):
                            pe.wait_ge(s_msg[k], 16 * i + 16 * (ITERS * layer + 1))
                            pe.wait_ge(s_sel, U * i + (tiles_before + k + 1))
                            if layer == 0:
                                pe.wait_ge(s_deg_sel, 2 * U * i + 2 * (k + 1))
                            for j in range(BANKS):
                                c = slice(j * STRIDE, (j + 1) * STRIDE)
                                last = T.matmul(acc[:, j, 0:STRIDE], msg[:, k, :], wide_sel[:, k % 2, c],
                                                start=False, stop=False, skip_group_check=True)
                                if layer == 0:
                                    last = T.matmul(ps[0:8, DEG:DEG + STRIDE], bank_col[:, j, :],
                                                    wide_deg[:, k % 2, c],
                                                    start=False, stop=False, skip_group_check=True)
                            last.then_inc(s_used, 1)

            def root_terms(layer, source):
                for j in range(BANKS):
                    T.matmul(acc[:, j, 0:STRIDE], root[layer][:, :], source[:, j * STRIDE:(j + 1) * STRIDE],
                             start=False, stop=False, skip_group_check=True)

            def close_sums():
                for j in range(BANKS):
                    close(j).then_inc(s_sum, 1)

            pe.wait_ge(s_tab_sb, FIRST_PIECE[1])
            for j in range(BANKS):
                clear(j)
            clear(BANKS, 8)
            root_terms(0, x_t)
            sums(0)
            close_sums()
            close(BANKS, 8).then_inc(s_deg_sum, 1)
            pe.wait_ge(s_h_dve, 2)
            pe.wait_ge(s_deg, 1)
            table(1, h_t, wall[1][:, :, :].rearrange("p r f -> p (r f)"),
                  lambda b: pe.wait_ge(s_h_act, min(((b + 1) * P - 1) // STRIDE + 1, BANKS)))
            pe.wait_ge(s_tab_sb, FIRST_PIECE[2])
            for j in range(BANKS):
                T.matmul(acc[:, j, :], row_sel[:, j, :], deg_sb[:, :], start=True, stop=True).then_inc(s_deg_mm, 1)
            for j in range(BANKS):
                pe.wait_ge(s_deg_b, j + 1)
                clear(j)
            root_terms(1, h_t)
            sums(1)
            close_sums()
            pe.wait_ge(s_z, 1)
            transposes(lambda b: z_t[:, b * P:(b + 1) * P], s_zn)
            transposes(lambda b: x2_nm[:, b, :], s_x2t_mm,
                       lambda b: pe.wait_ge(s_x2, min(4 * (b // 4) + 4, BLOCKS)) if b % 4 == 0 else None)
            pe.wait_ge(s_x2t, GROUPS)
            table(2, x2_t, wtop[:, :])
            pe.wait_ge(s_tab_sb, FIRST_PIECE[3])
            pe.wait_ge(s_b3, 1)
            for j in range(BANKS):
                pe.wait_ge(s_dx, j + 1)
                T.matmul(acc[:, j, :], b3_sel[:, j, :], deg_sb[:, :], start=True, stop=False, skip_group_check=True)
                T.matmul(acc[:, j, :], wbot[:, :], deg_x[:, j, :], start=False, stop=False, skip_group_check=True)
            sums(2)
            close_sums()
            pe.wait_ge(s_sig, BANKS + 1)
            transposes(lambda b: z_t[:, b * P:(b + 1) * P], s_sn)


def edges_by_tile(a):
    return np.ascontiguousarray(np.pad(np.asarray(a), (0, TILES * P - N_EDGES), mode="edge").reshape(TILES, P).T)


def kernel(x, src, dst, edge_type_4, edge_weight, L0_gnn_W1, L0_gnn_root1, L0_gnn_b1, L0_gnn_W2, L0_gnn_root2,
           L0_gnn_b2, L1_gnn_W, L1_gnn_b):
    import concourse.bacc as bacc
    from concourse.bass_utils import run_bass_kernel_spmd

    laid = {
        "x": np.pad(np.asarray(x), ((0, NP - N_NODES), (0, 0))),
        "src": edges_by_tile(src), "dst": edges_by_tile(dst),
        "types": edges_by_tile(edge_type_4), "weights": edges_by_tile(edge_weight),
        "w1": L0_gnn_W1, "root1": L0_gnn_root1, "b1": L0_gnn_b1,
        "w2": L0_gnn_W2, "root2": L0_gnn_root2, "b2": L0_gnn_b2, "w3": L1_gnn_W, "b3": L1_gnn_b,
    }
    nc = bacc.Bacc("TRN2", target_bir_lowering=False, num_devices=1)
    arrays, args = {}, []
    for name, a in laid.items():
        a = np.ascontiguousarray(a)
        arrays[f"in_{name}"] = a
        args.append(nc.dram_tensor(f"in_{name}", a.shape, mybir.dt.from_np(a.dtype), kind="ExternalInput").ap())
    args.append(nc.dram_tensor("out_y", (N_NODES, FEAT), mybir.dt.float32, kind="ExternalOutput").ap())
    build(nc, *args)
    r = run_bass_kernel_spmd(nc, [arrays], core_ids=[0])
    return r.results[0]["out_y"]
```

```python
import numpy as np
import concourse.bass as bass
from concourse import mybir
from contextlib import ExitStack

N_NODES, FEAT, N_EDGES, RELS = 3125, 128, 50000, 4
P = 128
BLOCKS = -(-N_NODES // P)
NP = BLOCKS * P
TILES = -(-N_EDGES // P)
LAST_EDGES = N_EDGES - (TILES - 1) * P
U = 17
ITERS = TILES // U
HALVES = [(0, 9), (9, U)]
assert ITERS * U == TILES
EARLY_PASSES = 2
EARLY = U * EARLY_PASSES
BATCH = 2
EARLY_BATCHES = EARLY // BATCH
AHEAD = 5
EARLY_LOOPS = (EARLY_BATCHES - AHEAD) // 2
EARLY_END = EARLY_PASSES + EARLY_LOOPS
FIRST_PASS = [EARLY_PASSES, 0, 0]
BEFORE = [0, ITERS - EARLY_PASSES, 2 * ITERS - EARLY_PASSES]
assert EARLY == BATCH * (AHEAD + 2 * EARLY_LOOPS)
BANK = 512
WIN = 64
STRIDE = BANK - WIN
BANKS = -(-N_NODES // STRIDE)
DEG = BANKS * BANK
ALLN = BANKS * STRIDE
READY = [j * STRIDE // P for j in range(BANKS)] + [BLOCKS]
FINAL = [9, 13, 16, 18, 20, 22, ITERS]
SECOND = [0, 0, 4, 9, 13, 17, 21, BLOCKS]
SPREAD = [(3, range(0, 4)), (6, range(4, BANKS))]
BEGUN = [[], [], [1], [2], [3], [], [4, 5, 6, 0]]
assert len(FINAL) == len(BEGUN) == BANKS and max(b - a for a, b in zip(READY, READY[1:])) <= 4
assert all(s <= r for s, r in zip(SECOND, READY))
FIRST_BATCH = 20
STAGES = 4
EARLY_BANKS = 3
BEGIN = [(EARLY_END, EARLY_BANKS), (EARLY_END + 1, EARLY_BANKS + 1)]
assert EARLY_BANKS + BATCH + 1 < BANKS and EARLY_END < FINAL[0]
X_PARTS = [(0, 4 * P), (4 * P, 12 * P), (12 * P, NP)]
EPS = 1e-5


def build(nc, x, x_rows, srcs, dsts, types, weights, w1, root1, b1, w2, root2, b2, w3, b3, out):
    fp32, bf16, i32 = mybir.dt.float32, mybir.dt.bfloat16, mybir.dt.int32
    ALU, ACT, AX = mybir.AluOpType, mybir.ActivationFunctionType, mybir.AxisListType

    tables = [nc.dram_tensor(f"table{n}", (NP, RELS * FEAT if n < 2 else FEAT), fp32, kind="Internal").ap()
              for n in range(3)]
    rows = [t.rearrange("n (r f) -> (n r) f", f=FEAT) for t in tables[:2]] + [tables[2]]

    with ExitStack() as ctx:
        def sb(name, shape, dt=fp32):
            return ctx.enter_context(nc.sbuf_tensor(name, shape, dt))

        def sem(name):
            return ctx.enter_context(nc.semaphore(name))

        src_i = sb("src_i", [P, TILES], i32)
        dst_i = sb("dst_i", [P, TILES], i32)
        typ_i = sb("typ_i", [P, TILES], i32)
        ew = sb("ew", [P, TILES])
        wall = [sb(f"wall{n}", [P, RELS, FEAT]) for n in range(2)]
        root = [sb(f"root{n}", [P, FEAT]) for n in range(2)]
        bias = [sb(f"bias{n}", [P, 1]) for n in range(2)]
        wtop = sb("wtop", [P, FEAT])
        wbot = sb("wbot", [P, FEAT])
        b3_all = sb("b3_all", [P, FEAT])
        iota = sb("iota", [P, ALLN])
        part = sb("part", [P, 1])
        ident = sb("ident", [P, P])
        ones_row = sb("ones_row", [1, P])
        zeros = sb("zeros", [P, BANK], bf16)
        row_sel = sb("row_sel", [8, BANKS, P])
        bank_col = sb("bank_col", [P, BANKS, 8], bf16)
        eps = sb("eps", [P, 1])
        dst_f = sb("dst_f", [P, TILES])
        base_f = sb("base_f", [P, TILES])
        rel_f = sb("rel_f", [P, TILES])
        bank_f = sb("bank_f", [P, TILES])
        idx12 = sb("idx12", [P, TILES], i32)
        w12 = sb("w12", [P, TILES])
        real = sb("real", [P, 1])
        col_i = sb("col_i", [1, TILES], i32)
        deg_col_i = sb("deg_col_i", [1, TILES], i32)
        col_t = sb("col_t", [1, TILES])
        ext = sb("ext", [P, 4])
        outside = sb("outside", [P, BANKS + len(BEGIN)])
        is_type = sb("is_type", [P, RELS, EARLY])
        ext_all = sb("ext_all", [P, 4])
        scale2 = sb("scale2", [P, 2])
        ok_f = sb("ok_f", [1, 2])
        ok_i = sb("ok_i", [1, 1], i32)
        idx_slot = sb("idx_slot", [P, U], i32)
        msg = sb("msg", [P, U, FEAT])
        sel = sb("sel", [P, U, WIN])
        hit_sel = sb("hit_sel", [P, U, WIN], bf16)
        deg_bank = sb("deg_bank", [P, U, 8], bf16)
        wide_sel = sb("wide_sel", [P, 2, ALLN])
        wide_deg = sb("wide_deg", [P, 2, ALLN], bf16)
        early_t = sb("early_t", [P, 2, BATCH * P])
        early_now = sb("early_now", [P, BATCH, FEAT])
        early_msg = sb("early_msg", [P, 2, BATCH, FEAT])
        early_sel = sb("early_sel", [P, 2, BATCH, WIN])
        early_hit_sel = sb("early_hit_sel", [P, 2, BATCH, WIN], bf16)
        early_deg_bank = sb("early_deg_bank", [P, 2, BATCH, 8], bf16)
        stage = sb("stage", [P, STAGES, BANK])
        x_t = sb("x_t", [P, NP])
        h_t = sb("h_t", [P, NP])
        z_t = sb("z_t", [P, NP])
        node_rows = sb("node_rows", [P, 2 * BLOCKS, FEAT])
        x2_nm = node_rows[:, 0:BLOCKS, :]
        u_nm = node_rows[:, BLOCKS:2 * BLOCKS, :]
        early = node_rows[:, 0:EARLY, :]
        x2_t = sb("x2_t", [P, NP])
        deg_sb = sb("deg_sb", [8, BANK])
        deg_x = sb("deg_x", [P, BANKS, STRIDE])
        shared = sb("shared", [P, BANKS - 1, WIN])
        shared2 = sb("shared2", [P, BANKS - 1, WIN])
        stats = sb("stats", [P, BLOCKS, 6])
        mv = sb("mv", [P, BLOCKS, 2])
        rstd = sb("rstd", [P, BLOCKS])
        nmr = sb("nmr", [P, BLOCKS])

        ps = ctx.enter_context(nc.psum_tensor("ps", [P, 8 * BANK], fp32))
        acc = ps[:, 0:BANKS * BANK].rearrange("p (j c) -> p j c", c=BANK)

        def tail_of(t):
            return t[:, 0:ALLN].rearrange("p (j c) -> p j c", c=STRIDE)[:, 1:BANKS, 0:WIN]

        s_ld_x = [sem(f"s_ld_x{n}") for n in range(len(X_PARTS))]
        s_ld_w1, s_ld_dst, s_ld_e, s_ld_w = sem("s_ld_w1"), sem("s_ld_dst"), sem("s_ld_e"), sem("s_ld_w")
        s_ld_src = sem("s_ld_src")
        s_clear, s_const, s_order = sem("s_clear"), sem("s_const"), sem("s_order")
        s_wide_iota = sem("s_wide_iota")
        s_early_now, s_early_part = sem("s_early_now"), sem("s_early_part")
        s_early_ahead, s_early_rest = sem("s_early_ahead"), sem("s_early_rest")
        s_early_tr, s_early_t, s_early_mm, s_early_msg, s_early_hit, s_early_sel, s_early_used = (
            sem("s_early_tr"), sem("s_early_t"), sem("s_early_mm"), sem("s_early_msg"), sem("s_early_hit"), sem("s_early_sel"),
            sem("s_early_used"))
        s_dstf, s_base_mm, s_ext, s_ext_all, s_edges = (
            sem("s_dstf"), sem("s_base_mm"), sem("s_ext"), sem("s_ext_all"), sem("s_edges"))
        s_tab_mm, s_tab_sb = sem("s_tab_mm"), sem("s_tab_sb")
        s_tab_out = [sem(f"s_tab_out{n}") for n in range(STAGES)]
        s_idx, s_gate = sem("s_idx"), sem("s_gate")
        s_msg = [sem(f"s_msg{k}") for k in range(U)]
        s_hit, s_sel, s_used = sem("s_hit"), sem("s_sel"), sem("s_used")
        s_sum, s_deg_sum = sem("s_sum"), sem("s_deg_sum")
        s_deg, s_deg_mm, s_deg_b = sem("s_deg"), sem("s_deg_mm"), sem("s_deg_b")
        s_bank_read = sem("s_bank_read")
        s_h_act, s_h_dve = sem("s_h_act"), sem("s_h_dve")
        s_z, s_zn, s_stat, s_std, s_rstd, s_x2 = (
            sem("s_z"), sem("s_zn"), sem("s_stat"), sem("s_std"), sem("s_rstd"), sem("s_x2"))
        s_x2t_mm, s_x2t, s_dx, s_sp, s_u = sem("s_x2t_mm"), sem("s_x2t"), sem("s_dx"), sem("s_sp"), sem("s_u")
        s_ov, s_sig, s_sn, s_stat2, s_std2, s_rstd2, s_y, s_out = (
            sem("s_ov"), sem("s_sig"), sem("s_sn"), sem("s_stat2"), sem("s_std2"), sem("s_rstd2"),
            sem("s_y"), sem("s_out"))
        block = ctx.enter_context(nc.Block())

        def stops(layer):
            found = [(p, "final", j) for j, p in enumerate(FINAL)]
            return sorted(found + [(p, "spread", banks) for p, banks in SPREAD] * (layer == 1), key=lambda s: s[0])

        FIRST_PIECE = [0, BLOCKS, 2 * BLOCKS, 2 * BLOCKS + BANKS]
        def table_done(layer, slot):
            return 16 * len([n for n in range(FIRST_PIECE[layer + 1]) if n % STAGES == slot])

        def shared_norm(lo, hi):
            return lo + (hi - lo + 1) // 2

        def z_block(j, b):
            lo, mid = READY[j], shared_norm(READY[j], READY[j + 1])
            column = DEG + (b - lo) * P if b < mid else (b - mid) * P
            return ps[:, column:column + P]

        @block.sync
        def _(sp):
            sp.dma_start(wall[0][:, :, :], w1.rearrange("r i o -> i r o")).then_inc(s_ld_w1, 16)
            for n, (lo, hi) in enumerate(X_PARTS):
                sp.dma_start(x_t[:, lo:hi], x[:, lo:hi]).then_inc(s_ld_x[n], 16)
                if n == 0:
                    sp.dma_start(dst_i[:, :], dsts).then_inc(s_ld_dst, 16)
            sp.dma_start(root[0][:, :], root1).then_inc(s_ld_w, 16)
            sp.dma_start(bias[0][:, :], b1.rearrange("(f a) -> f a", a=1)).then_inc(s_ld_w, 16)
            sp.dma_start(wall[1][:, :, :], w2.rearrange("r i o -> i r o")).then_inc(s_ld_w, 16)
            sp.dma_start(root[1][:, :], root2).then_inc(s_ld_w, 16)
            sp.dma_start(bias[1][:, :], b2.rearrange("(f a) -> f a", a=1)).then_inc(s_ld_w, 16)
            sp.dma_start(wtop[:, :], w3[0:FEAT, :]).then_inc(s_ld_w, 16)
            sp.dma_start(wbot[:, :], w3[FEAT:2 * FEAT, :]).then_inc(s_ld_w, 16)
            sp.dma_start(b3_all[:, :], b3.rearrange("(a f) -> a f", a=1).to_broadcast([P, FEAT])).then_inc(s_ld_w, 16)
            for layer in range(3):
                for n in range(FIRST_PIECE[layer], FIRST_PIECE[layer + 1]):
                    sp.wait_ge(s_tab_sb, n + 1)
                    b = n - FIRST_PIECE[layer]
                    if layer < 2:
                        dest, piece = tables[layer][b * P:(b + 1) * P, :], stage[:, n % STAGES, :]
                    else:
                        dest = tables[2][READY[b] * P:READY[b + 1] * P, :].rearrange("(q p) f -> p q f", p=P)
                        piece = stage[:, n % STAGES, 0:(READY[b + 1] - READY[b]) * FEAT].rearrange("p (q f) -> p q f", f=FEAT)
                    sp.dma_start(dest, piece).then_inc(s_tab_out[n % STAGES], 16)
            count = 0
            for j in range(BANKS):
                sp.wait_ge(s_y, READY[j + 1])
                lo, hi = READY[j], min(READY[j + 1], N_NODES // P)
                sp.dma_start(out[lo * P:hi * P, :].rearrange("(b p) f -> p b f", p=P),
                             x2_nm[:, lo:hi, :]).then_inc(s_out, 16)
                count += 1
            sp.dma_start(out[(BLOCKS - 1) * P:N_NODES, :],
                         x2_nm[0:N_NODES - (BLOCKS - 1) * P, BLOCKS - 1, :]).then_inc(s_out, 16)
            count += 1
            sp.wait_ge(s_out, 16 * count)

        @block.gpsimd
        def _(pool):
            nc.gpsimd.memset(ident[:, :], 0.0).then_inc(s_clear, 1)
            nc.gpsimd.memset(row_sel[:, :, :], 0.0).then_inc(s_clear, 1)
            nc.gpsimd.iota(iota[:, 0:WIN], [[1, WIN]], base=0, channel_multiplier=0,
                           allow_small_or_imprecise_dtypes=True).then_inc(s_const, 1)
            nc.gpsimd.iota(part[:, :], [[0, 1]], base=0, channel_multiplier=1,
                           allow_small_or_imprecise_dtypes=True).then_inc(s_const, 1)
            pool.wait_ge(s_clear, 2)
            nc.gpsimd.affine_select(out=ident[:, :], in_=ident[:, :], compare_op=ALU.not_equal, fill=1.0,
                                    base=0, pattern=[[-1, P]], channel_multiplier=1).then_inc(s_const, 1)
            nc.gpsimd.affine_select(out=row_sel[:, :, :], in_=row_sel[:, :, :], compare_op=ALU.not_equal,
                                    fill=1.0, base=0, pattern=[[-1, BANKS], [0, P]],
                                    channel_multiplier=1).then_inc(s_const, 1)
            def early_rows(lo, hi, done):
                for t in range(lo, hi):
                    pool.indirect_dma_start(early[:, t, :], None, x_rows,
                                            bass.IndirectOffsetOnAxis(src_i[:, t:t + 1], 0)).then_inc(done, 16)

            pool.wait_ge(s_ld_src, 16)
            early_rows(0, AHEAD * BATCH, s_early_ahead)
            early_rows(AHEAD * BATCH, U, s_early_rest)
            pool.wait_ge(s_ext, 4)
            nc.gpsimd.partition_all_reduce(ext_all[:, :], ext[:, :], P, bass.bass_isa.ReduceOp.max)\
                .then_inc(s_ext_all, 1)
            early_rows(U, EARLY, s_early_rest)
            for layer in range(3):
                for n in range(STAGES):
                    pool.wait_ge(s_tab_out[n], table_done(layer, n))
                with pool.Fori(0, ITERS - FIRST_PASS[layer]) as i:
                    for half, (lo, hi) in enumerate(HALVES):
                        pool.wait_ge(s_idx, 2 * i + (2 * BEFORE[layer] + half + 1))
                        pool.sem_inc(s_gate, 1)
                        for k in range(lo, hi):
                            pool.indirect_dma_start(
                                msg[:, k, :], None, rows[layer],
                                bass.IndirectOffsetOnAxis(idx_slot[:, k:k + 1], 0)).then_inc(s_msg[k], 16)

        @block.scalar
        def _(act):
            act.dma_start(src_i[:, :], srcs).then_inc(s_ld_src, 16)
            act.dma_start(typ_i[:, :], types).then_inc(s_ld_e, 16)
            act.dma_start(ew[:, :], weights).then_inc(s_ld_e, 16)

            def table_piece(n):
                bank = n % 2
                act.wait_ge(s_tab_mm, n + 1)
                if n >= STAGES:
                    act.wait_ge(s_tab_out[n % STAGES], 16 * (n // STAGES))
                nc.scalar.copy(stage[:, n % STAGES, :], ps[:, bank * BANK:(bank + 1) * BANK])\
                    .then_inc(s_tab_sb, 1)

            def half_indices(layer, i, lo, hi):
                table = idx12 if layer < 2 else src_i
                act.wait_ge(s_used, U * i + (U * BEFORE[layer] + hi))
                nc.scalar.copy(idx_slot[:, lo:hi], table[:, bass.ds(U * i + (U * FIRST_PASS[layer] + lo), hi - lo)])\
                    .then_inc(s_idx, 1)

            def indices(layer, start, end):
                with act.Fori(start - FIRST_PASS[layer], end - FIRST_PASS[layer]) as i:
                    for lo, hi in HALVES:
                        half_indices(layer, i, lo, hi)

            def early_batch(batch, slot):
                early_rows(batch)
                early_transposed(batch, slot)

            def early_rows(batch):
                nc.scalar.copy(early_now[:, :, :], early[:, bass.ds(batch * BATCH, BATCH), :]).then_inc(s_early_now, 1)

            def early_transposed(batch, slot):
                act.wait_ge(s_early_tr, batch + 1)
                nc.scalar.copy(early_t[:, slot, :], acc[:, BANKS - 1, 0:BATCH * P]).then_inc(s_early_t, 1)

            for n in range(BLOCKS):
                if n == FIRST_BATCH - 1:
                    act.wait_ge(s_early_ahead, 16 * AHEAD * BATCH)
                    early_rows(0)
                elif n == FIRST_BATCH:
                    early_transposed(0, 0)
                table_piece(n)

            def softplus():
                act.wait_ge(s_x2, BLOCKS)
                nc.scalar.activation(u_nm[:, :, :], x2_nm[:, :, :], ACT.Exp).then_inc(s_sp, 1)
                act.wait_ge(s_sp, 1)
                nc.scalar.activation(u_nm[:, :, :], u_nm[:, :, :], ACT.Ln, bias=1.0).then_inc(s_sp, 1)

            def norm(j, stat, std, ready, source, done):
                lo, hi = READY[j], READY[j + 1]
                act.wait_ge(stat, j + 1)
                nc.scalar.activation(rstd[:, lo:hi], mv[:, lo:hi, 1], ACT.Sqrt, bias=eps[:, 0:1]).then_inc(std, 1)
                act.wait_ge(ready, j + 1)
                for b in range(lo, shared_norm(lo, hi)):
                    nc.scalar.activation(x2_nm[:, b, :], source(b), ACT.Identity,
                                         bias=nmr[:, b:b + 1], scale=rstd[:, b:b + 1]).then_inc(done, 1)

            def final(layer, j):
                lo = 0 if j == 0 else WIN
                if layer == 0:
                    act.wait_ge(s_bank_read, j + 1)
                    nc.scalar.activation(h_t[:, j * STRIDE + lo:(j + 1) * STRIDE], acc[:, j, lo:STRIDE],
                                         ACT.Relu, bias=bias[0][:, 0:1]).then_inc(s_h_act, 1)
                    for b in range(SECOND[j], SECOND[j + 1]):
                        table_piece(BLOCKS + b)
                elif layer == 1:
                    norm(j, s_stat, s_std, s_rstd,
                         lambda b: z_block(j, b), s_x2)
                else:
                    act.wait_ge(s_ov, j + 1)
                    if j > 0:
                        nc.scalar.activation(z_t[:, j * STRIDE:j * STRIDE + WIN], shared2[:, j - 1, :],
                                             ACT.Sigmoid).then_inc(s_sig, 1)
                    nc.scalar.activation(z_t[:, j * STRIDE + lo:(j + 1) * STRIDE], acc[:, j, lo:STRIDE],
                                         ACT.Sigmoid).then_inc(s_sig, 1)
                    norm(j, s_stat2, s_std2, s_rstd2, lambda b: u_nm[:, b, :], s_y)

            def spread(banks):
                for d in banks:
                    act.wait_ge(s_deg_mm, d + 1)
                    nc.scalar.copy(deg_x[:, d, :], ps[:, DEG:DEG + STRIDE]).then_inc(s_deg_b, 1)

            act.wait_ge(s_edges, 3)
            sorted_flag = act.value_load(ok_i[0:1, 0:1], min_val=0, max_val=1)
            for layer in range(3):
                if layer == 0:
                    indices(0, EARLY_PASSES, EARLY_PASSES + 1)
                with act.If(sorted_flag == 1):
                    at = 0
                    if layer == 0:
                        for b in range(1, AHEAD):
                            early_batch(b, b % 2)
                        act.wait_ge(s_early_rest, 16 * (EARLY - AHEAD * BATCH))
                        with act.Fori(0, EARLY_LOOPS) as i:
                            for half, (lo, hi) in enumerate(HALVES):
                                half_indices(0, i + 1, lo, hi)
                                early_batch(2 * i + (AHEAD + half), (AHEAD + half) % 2)
                        at = EARLY_END + 1
                    if layer == 2:
                        indices(2, 0, 2)
                        softplus()
                        at = 2
                    for passes, what, arg in stops(layer):
                        to = min(passes + 1, ITERS)
                        if to > at:
                            indices(layer, at, to)
                        at = to
                        final(layer, arg) if what == "final" else spread(arg)
                with act.Else():
                    if layer == 0:
                        act.wait_ge(s_early_rest, 16 * (EARLY - AHEAD * BATCH))
                        for b in range(1, EARLY_BATCHES):
                            early_batch(b, b % 2)
                    elif layer == 2:
                        indices(2, 0, 2)
                        softplus()
                    indices(layer, [EARLY_PASSES + 1, 0, 2][layer], ITERS)
                    for _, what, arg in stops(layer):
                        final(layer, arg) if what == "final" else spread(arg)

        @block.vector
        def _(dve):
            chain = [0]

            def link(ins):
                chain[0] += 1
                ins.then_inc(s_order, 1)
                dve.wait_ge(s_order, chain[0])

            V = nc.vector
            V.memset(ones_row[:, :], 1.0).then_inc(s_const, 1)
            V.memset(zeros[:, :], 0.0).then_inc(s_const, 1)
            V.memset(eps[:, :], EPS).then_inc(s_const, 1)
            link(V.memset(bank_col[:, :, :], 0.0))
            V.memset(bank_col[:, :, :].rearrange("p a b -> p (a b)")[:, 0:8 * BANKS:9], 1.0).then_inc(s_const, 1)
            V.memset(h_t[:, ALLN:NP], 0.0).then_inc(s_const, 1)
            V.memset(z_t[:, ALLN:NP], 0.0).then_inc(s_const, 1)
            dve.wait_ge(s_ld_dst, 16)
            V.tensor_copy(dst_f[:, :], dst_i[:, :]).then_inc(s_dstf, 1)
            dve.wait_ge(s_ld_src, 16)
            dve.wait_ge(s_ld_e, 32)
            link(V.scalar_tensor_tensor(idx12[:, :], src_i[:, :], float(RELS), typ_i[:, :], ALU.mult, ALU.add))
            V.reduce_max(ext[:, 0:1], ew[:, :], axis=AX.X).then_inc(s_ext, 1)
            V.tensor_reduce(ext[:, 1:2], ew[:, :], AX.X, ALU.min, negate=True).then_inc(s_ext, 1)
            dve.wait_ge(s_base_mm, 1)
            link(V.tensor_copy(base_f[:, :], ps[:, DEG:DEG + TILES]))
            link(V.tensor_tensor(rel_f[:, :], dst_f[:, :], base_f[:, :], ALU.subtract))
            V.reduce_max(ext[:, 2:3], rel_f[:, :], axis=AX.X).then_inc(s_ext, 1)
            link(V.tensor_reduce(outside[:, BANKS - 1:BANKS], rel_f[:, :], AX.X, ALU.min, negate=True))
            for j in range(BANKS - 1):
                link(V.tensor_reduce(outside[:, j:j + 1], dst_f[:, U * FINAL[j]:TILES], AX.X, ALU.min, negate=True))
                link(V.tensor_scalar_add(outside[:, j:j + 1], outside[:, j:j + 1], float(STRIDE * (j + 1))))
            for n, (passes, banks) in enumerate(BEGIN):
                above = outside[:, BANKS + n:BANKS + n + 1]
                link(V.reduce_max(above, dst_f[:, 0:U * passes], axis=AX.X))
                link(V.tensor_scalar_add(above, above, float(1 - STRIDE * banks)))
            V.reduce_max(ext[:, 3:4], outside[:, :], axis=AX.X).then_inc(s_ext, 1)
            for r in range(RELS):
                V.tensor_single_scalar(is_type[:, r, :], typ_i[:, 0:EARLY], float(r), ALU.is_equal)\
                    .then_inc(s_order, 1)
                chain[0] += 1
            link(V.tensor_single_scalar(bank_f[:, :], base_f[:, :], float(STRIDE), ALU.is_ge))
            for j in range(2, BANKS):
                link(V.scalar_tensor_tensor(bank_f[:, :], base_f[:, :], float(STRIDE * j), bank_f[:, :],
                                            ALU.is_ge, ALU.add))
            V.scalar_tensor_tensor(col_i[:, :], bank_f[0:1, :], float(WIN), base_f[0:1, :], ALU.mult, ALU.add)\
                .then_inc(s_edges, 1)
            link(V.scalar_tensor_tensor(col_t[:, :], bank_f[0:1, :], -float(STRIDE), base_f[0:1, :],
                                        ALU.mult, ALU.add))
            V.tensor_scalar_add(deg_col_i[:, :], col_t[:, :], float(DEG)).then_inc(s_edges, 1)
            dve.wait_ge(s_const, 10)
            link(V.tensor_single_scalar(real[:, :], part[:, :], float(LAST_EDGES), ALU.is_lt))
            for dest in (rel_f, dst_f):
                link(V.scalar_tensor_tensor(dest[:, TILES - 1:TILES], dest[:, TILES - 1:TILES], 1.0, real[:, :],
                                            ALU.add, ALU.mult))
                link(V.tensor_scalar_add(dest[:, TILES - 1:TILES], dest[:, TILES - 1:TILES], -1.0))
            dve.wait_ge(s_ext_all, 1)
            link(V.tensor_tensor(scale2[:, 0:1], ext_all[:, 0:1], ext_all[:, 1:2], ALU.add))
            link(V.tensor_scalar_add(scale2[:, 0:1], scale2[:, 0:1], 1e-8))
            link(V.reciprocal(scale2[:, 1:2], scale2[:, 0:1]))
            link(V.tensor_scalar(w12[:, :], ew[:, :], ext_all[:, 1:2], scale2[:, 1:2], ALU.add, ALU.mult))
            link(V.tensor_single_scalar(ok_f[:, 0:1], ext_all[0:1, 2:3], float(WIN), ALU.is_lt))
            link(V.tensor_single_scalar(ok_f[:, 1:2], ext_all[0:1, 3:4], 0.0, ALU.is_le))
            link(V.tensor_tensor(ok_i[:, :], ok_f[:, 0:1], ok_f[:, 1:2], ALU.mult))
            dve.wait_ge(s_ld_w, 128)
            V.engine_nop().then_inc(s_edges, 1)
            sorted_flag = dve.value_load(ok_i[0:1, 0:1], min_val=0, max_val=1)

            def select(layer, t, n, sel_to, hit_to, bank_to, hit, hits, done):
                tiles, wide = bass.ds(t, n), [P, n, WIN]
                columns = iota[:, 0:WIN].unsqueeze(1).to_broadcast(wide)
                rel = rel_f[:, tiles].unsqueeze(2).to_broadcast(wide)
                if layer == 2:
                    V.tensor_tensor(sel_to, columns, rel, ALU.is_equal).then_inc(done, 1)
                    return
                V.tensor_tensor(hit_to, columns, rel, ALU.is_equal).then_inc(hit, 1)
                if layer == 0:
                    V.tensor_tensor(bank_to, iota[:, 0:8].unsqueeze(1).to_broadcast([P, n, 8]),
                                    bank_f[:, tiles].unsqueeze(2).to_broadcast([P, n, 8]), ALU.is_equal)\
                        .then_inc(hit, 1)
                dve.wait_ge(hit, hits)
                V.tensor_tensor(sel_to, hit_to, w12[:, tiles].unsqueeze(2).to_broadcast(wide), ALU.mult)\
                    .then_inc(done, 1)

            def half_near(layer, i, half):
                lo, hi = HALVES[half]
                dve.wait_ge(s_used, U * i + (U * BEFORE[layer] + hi))
                hits = 4 * i + 2 * (half + 1) if layer == 0 else 2 * i + (4 * BEFORE[1] + half + 1)
                select(layer, U * i + (U * FIRST_PASS[layer] + lo), hi - lo, sel[:, lo:hi, :], hit_sel[:, lo:hi, :],
                       deg_bank[:, lo:hi, :], s_hit, hits, s_sel)

            def near(layer, start, end):
                with dve.Fori(start - FIRST_PASS[layer], end - FIRST_PASS[layer]) as i:
                    for half in range(2):
                        half_near(layer, i, half)

            def early_place(batch, m):
                return early[:, bass.ds(batch * BATCH + m, 1), :].rearrange("p a f -> p (a f)")

            def early_messages(batch, place):
                for m in range(BATCH):
                    dve.wait_ge(s_early_mm, BATCH * batch + (m + 1))
                    for r in range(RELS):
                        holds = is_type[:, r, bass.ds(batch * BATCH + m, 1)]
                        product = acc[:, EARLY_BANKS + m, r * FEAT:(r + 1) * FEAT]
                        if r == 0:
                            last = V.tensor_scalar(place(batch, m), product, holds, None, ALU.mult)
                        else:
                            dve.wait_ge(s_early_part, (RELS - 1) * BATCH * batch + ((RELS - 1) * m + r))
                            last = V.scalar_tensor_tensor(place(batch, m), product, holds, place(batch, m),
                                                          ALU.mult, ALU.add)
                        last.then_inc(s_early_msg if r == RELS - 1 else s_early_part, 1)

            def early_near(batch, slot):
                dve.wait_ge(s_early_used, BATCH * batch + (U - BATCH))
                select(0, batch * BATCH, BATCH, early_sel[:, slot, :, :], early_hit_sel[:, slot, :, :],
                       early_deg_bank[:, slot, :, :], s_early_hit, 2 * batch + 2, s_early_sel)
                early_messages(batch, lambda batch, m: early_msg[:, slot, m, :])

            def wide(layer, early_tiles=False):
                first = 0 if early_tiles else U * FIRST_PASS[layer]
                before = 0 if early_tiles else U * BEFORE[layer]
                used = s_early_used if early_tiles else s_used
                with dve.Fori(0, EARLY_PASSES if early_tiles else ITERS - FIRST_PASS[layer]) as i:
                    for k in range(U):
                        done = k if k == 0 else k - 1
                        dve.wait_ge(used, U * i + (before + U + done))
                        if early_tiles:
                            V.tensor_copy(early_msg[:, 0, k % 2, :].unsqueeze(1), early[:, bass.ds(U * i + k, 1), :])\
                                .then_inc(s_early_sel, 1)
                        dst = dst_f[:, bass.ds(U * i + (first + k), 1)]
                        if layer == 2:
                            V.tensor_scalar(wide_sel[:, k % 2, :], iota[:, :], dst, None, ALU.is_equal)\
                                .then_inc(s_sel, 1)
                        else:
                            V.tensor_scalar(wide_sel[:, k % 2, :], iota[:, :], dst,
                                            w12[:, bass.ds(U * i + (first + k), 1)], ALU.is_equal, ALU.mult)\
                                .then_inc(s_early_sel if early_tiles else s_sel, 1)
                        if layer == 0:
                            V.tensor_scalar(wide_deg[:, k % 2, :], iota[:, :], dst, None, ALU.is_equal)\
                                .then_inc(s_early_hit if early_tiles else s_hit, 1)

            def statistics(j, source, done):
                lo, hi = READY[j], READY[j + 1]
                for b in range(lo, hi):
                    last = V.bn_stats(stats[:, b, :], source(b))
                    if b < hi - 1:
                        last.then_inc(s_order, 1)
                        chain[0] += 1
                link(last)
                for b in range(lo, hi):
                    last = V.bn_aggr(mv[:, b, :], stats[:, b, :])
                    if b < hi - 1:
                        last.then_inc(s_order, 1)
                        chain[0] += 1
                last.then_inc(done, 1)

            def norm(j, std, ready, source, done):
                lo, hi = READY[j], READY[j + 1]
                dve.wait_ge(std, j + 1)
                link(V.reciprocal(rstd[:, lo:hi], rstd[:, lo:hi]))
                V.scalar_tensor_tensor(nmr[:, lo:hi], mv[:, lo:hi, 0], -1.0, rstd[:, lo:hi],
                                       ALU.mult, ALU.mult).then_inc(ready, 1)
                dve.wait_ge(ready, j + 1)
                for b in range(shared_norm(lo, hi), hi):
                    V.tensor_scalar(x2_nm[:, b, :], source(b), rstd[:, b:b + 1], nmr[:, b:b + 1], ALU.mult, ALU.add)\
                        .then_inc(done, 1)

            def final(layer, j):
                dve.wait_ge(s_sum, BANKS * layer + j + 1)
                nodes = slice(j * STRIDE, (j + 1) * STRIDE)
                first = slice(j * STRIDE, j * STRIDE + WIN)
                common = acc[:, j, STRIDE:BANK]
                if layer == 0:
                    if j < BANKS - 1:
                        last = V.tensor_scalar(shared[:, j, :], common, bias[0][:, 0:1], None, ALU.add)
                        if j == 0:
                            last.then_inc(s_bank_read, 1)
                            dve.wait_ge(s_bank_read, 1)
                        else:
                            link(last)
                    if j > 0:
                        V.tensor_tensor(shared2[:, j - 1, :], acc[:, j, 0:WIN], shared[:, j - 1, :], ALU.add)\
                            .then_inc(s_bank_read, 1)
                        dve.wait_ge(s_bank_read, j + 1)
                        V.tensor_scalar(h_t[:, first], shared2[:, j - 1, :], 0.0, None, ALU.max).then_inc(s_h_dve, 1)
                elif layer == 1:
                    if j < BANKS - 1:
                        link(V.tensor_copy(shared[:, j, :], common))
                    last = V.scalar_tensor_tensor(z_t[:, nodes], acc[:, j, 0:STRIDE], bias[1][:, 0:1],
                                                  x_t[:, nodes], ALU.add, ALU.add)
                    if j > 0:
                        link(last)
                        last = V.tensor_tensor(z_t[:, first], z_t[:, first], shared[:, j - 1, :], ALU.add)
                    last.then_inc(s_z, 1)
                    dve.wait_ge(s_zn, j + 1)
                    statistics(j, lambda b: z_block(j, b), s_stat)
                    norm(j, s_std, s_rstd, lambda b: z_block(j, b), s_x2)
                    dve.wait_ge(s_x2t_mm, j + 1)
                    V.tensor_copy(x2_t[:, READY[j] * P:READY[j + 1] * P], ps[:, 0:(READY[j + 1] - READY[j]) * P])\
                        .then_inc(s_x2t, 1)
                    n, k = 2 * BLOCKS + j, READY[j + 1] - READY[j]
                    dve.wait_ge(s_tab_mm, n + 1)
                    dve.wait_ge(s_tab_out[n % STAGES], 16 * (n // STAGES))
                    V.tensor_tensor(stage[:, n % STAGES, 0:k * FEAT].rearrange("p (q f) -> p q f", f=FEAT),
                                    ps[:, DEG:DEG + k * FEAT].rearrange("p (q f) -> p q f", f=FEAT),
                                    b3_all[:, :].unsqueeze(1).to_broadcast([P, k, FEAT]), ALU.add)\
                        .then_inc(s_tab_sb, 1)
                    for d in BEGUN[j]:
                        dve.wait_ge(s_deg_b, d + 1)
                        dve.wait_ge(s_x2t, j + 1)
                        V.tensor_tensor(deg_x[:, d, :], deg_x[:, d, :], x2_t[:, d * STRIDE:(d + 1) * STRIDE],
                                        ALU.mult).then_inc(s_dx, 1)
                else:
                    if j == 0:
                        dve.wait_ge(s_sp, 2)
                        link(V.tensor_tensor(u_nm[:, :, :], u_nm[:, :, :], x2_nm[:, :, :], ALU.add))
                    if j < BANKS - 1:
                        last = V.tensor_copy(shared[:, j, :], common)
                        if j == 0:
                            last.then_inc(s_ov, 1)
                        else:
                            link(last)
                    if j > 0:
                        V.tensor_tensor(shared2[:, j - 1, :], acc[:, j, 0:WIN], shared[:, j - 1, :], ALU.add)\
                            .then_inc(s_ov, 1)
                    dve.wait_ge(s_sn, j + 1)
                    lo, hi = READY[j], READY[j + 1]
                    link(V.tensor_tensor(u_nm[:, lo:hi, :],
                                         ps[:, DEG:DEG + (hi - lo) * P].rearrange("p (b f) -> p b f", f=P),
                                         u_nm[:, lo:hi, :], ALU.add))
                    statistics(j, lambda b: u_nm[:, b, :], s_stat2)
                    norm(j, s_std2, s_rstd2, lambda b: u_nm[:, b, :], s_y)

            wide_iotas = 0
            for layer in range(3):
                chain_before = chain[0]
                with dve.If(sorted_flag == 1):
                    at = 0
                    if layer == 0:
                        for b in range(AHEAD - 1):
                            early_near(b, b % 2)
                        half_near(0, 0, 0)
                        with dve.Fori(0, EARLY_LOOPS) as i:
                            half_near(0, i, 1)
                            early_near(2 * i + (AHEAD - 1), (AHEAD - 1) % 2)
                            half_near(0, i + 1, 0)
                            early_near(2 * i + AHEAD, AHEAD % 2)
                        early_near(EARLY_BATCHES - 1, (EARLY_BATCHES - 1) % 2)
                        half_near(0, EARLY_LOOPS, 1)
                        at = EARLY_END + 1
                    for j in range(BANKS):
                        to = min(FINAL[j] + 1, ITERS)
                        if to > at:
                            near(layer, at, to)
                        at = to
                        final(layer, j)
                with dve.Else():
                    chain[0] = chain_before
                    if layer == 0:
                        width = WIN
                        while width < ALLN:
                            more = min(width, ALLN - width)
                            V.tensor_scalar_add(iota[:, width:width + more], iota[:, 0:more], float(width))\
                                .then_inc(s_wide_iota, 1)
                            width += more
                            wide_iotas += 1
                            dve.wait_ge(s_wide_iota, wide_iotas)
                        for b in range(EARLY_BATCHES):
                            early_messages(b, early_place)
                        wide(0, early_tiles=True)
                        dve.wait_ge(s_early_used, U + EARLY)
                    wide(layer)
                    for j in range(BANKS):
                        final(layer, j)
                if layer == 0:
                    dve.wait_ge(s_deg_sum, 1)
                    V.tensor_copy(deg_sb[:, :], ps[0:8, DEG:DEG + BANK]).then_inc(s_deg, 1)
                elif layer == 1:
                    dve.wait_ge(s_x2, BLOCKS)

        @block.tensor
        def _(pe):
            T = nc.tensor

            def table_product(n, source, weight):
                b = n % BLOCKS
                if n >= 2:
                    pe.wait_ge(s_tab_sb, n - 1)
                T.matmul(ps[:, (n % 2) * BANK:(n % 2 + 1) * BANK], source[:, b * P:(b + 1) * P],
                         weight[:, :, :].rearrange("p r f -> p (r f)"), start=True, stop=True).then_inc(s_tab_mm, 1)

            def clear(j, rows=P):
                T.matmul(ps[0:rows, j * BANK:(j + 1) * BANK], zeros[:, 0:rows], zeros[:, :], start=True, stop=False,
                         skip_group_check=True)

            def close(j, rows=P):
                return T.matmul(ps[0:rows, j * BANK:(j + 1) * BANK], zeros[:, 0:rows], zeros[:, :], start=False,
                                stop=True, skip_group_check=True)

            def transposes(source, lo, hi, column):
                for b in range(lo, hi):
                    last = T.transpose(ps[:, column + (b - lo) * P:column + (b - lo + 1) * P], source(b), ident[:, :])
                return last

            def bases():
                pe.wait_ge(s_const, 10)
                pe.wait_ge(s_dstf, 1)
                T.matmul(ps[:, DEG:DEG + TILES], ones_row[:, :], dst_f[0:1, :], start=True, stop=True)\
                    .then_inc(s_base_mm, 1)

            def early_transposes(batch, first=False):
                pe.wait_ge(s_early_now, batch + 1)
                if not first:
                    pe.wait_ge(s_early_t, batch)
                for m in range(BATCH):
                    last = T.transpose(acc[:, BANKS - 1, m * P:(m + 1) * P], early_now[:, m, :], ident[:, :])
                last.then_inc(s_early_tr, 1)

            def early_products(batch, slot, first=False):
                pe.wait_ge(s_early_t, batch + 1)
                for m in range(BATCH):
                    if not first:
                        pe.wait_ge(s_early_msg, BATCH * batch + (m + 1 - BATCH))
                    T.matmul(acc[:, EARLY_BANKS + m, :], early_t[:, slot, m * P:(m + 1) * P],
                             wall[0][:, :, :].rearrange("p r f -> p (r f)"), start=True, stop=True)\
                        .then_inc(s_early_mm, 1)

            pe.sem_inc(s_used, U)
            pe.sem_inc(s_early_used, U)
            pe.wait_ge(s_ld_w1, 16)
            for n in range(BLOCKS):
                for part, (lo, hi) in enumerate(X_PARTS):
                    if n * P == lo:
                        pe.wait_ge(s_ld_x[part], 16)
                if n == FIRST_BATCH:
                    early_transposes(0, first=True)
                elif n == FIRST_BATCH + 1:
                    early_products(0, 0, first=True)
                table_product(n, x_t, wall[0])
                if n == 3:
                    bases()
            pe.wait_ge(s_ld_w, 128)
            pe.wait_ge(s_edges, 3)
            sorted_flag = pe.value_load(ok_i[0:1, 0:1], min_val=0, max_val=1)

            def registers(values, least, most):
                return nc.values_load_multi_w_load_instructions(
                    values, engines=[mybir.EngineType.PE], min_val=least, max_val=most,
                    skip_runtime_bounds_check_because="worked out from destinations, which are nodes")[1]

            def root_term(layer, source, j):
                clear(j)
                T.matmul(acc[:, j, 0:STRIDE], root[layer][:, :], source[:, j * STRIDE:(j + 1) * STRIDE],
                         start=False, stop=False, skip_group_check=True)

            def half_near(layer, i, half):
                lo, hi = HALVES[half]
                first = U * i + (U * FIRST_PASS[layer] + lo)
                cols = registers(col_i[0:1, bass.ds(first, hi - lo)], 0, BANKS * BANK - WIN)
                if layer == 0:
                    deg_cols = registers(deg_col_i[0:1, bass.ds(first, hi - lo)], DEG, 8 * BANK - WIN)
                pe.wait_ge(s_sel, 2 * i + (2 * BEFORE[layer] + half + 1))
                for k in range(lo, hi):
                    pe.wait_ge(s_msg[k], 16 * i + 16 * (BEFORE[layer] + 1))
                    last = T.matmul(ps[:, bass.ds(cols[k - lo], WIN)], msg[:, k, :], sel[:, k, :],
                                    start=False, stop=False, skip_group_check=True)
                    if layer == 0:
                        last = T.matmul(ps[0:8, bass.ds(deg_cols[k - lo], WIN)], deg_bank[:, k, :],
                                        hit_sel[:, k, :], start=False, stop=False, skip_group_check=True)
                    last.then_inc(s_used, 1)

            def near(layer, start, end):
                with pe.Fori(start - FIRST_PASS[layer], end - FIRST_PASS[layer]) as i:
                    for half in range(2):
                        half_near(layer, i, half)

            def early_sums(batch, slot):
                cols = registers(col_i[0:1, bass.ds(batch * BATCH, BATCH)], 0, BANKS * BANK - WIN)
                deg_cols = registers(deg_col_i[0:1, bass.ds(batch * BATCH, BATCH)], DEG, 8 * BANK - WIN)
                pe.wait_ge(s_early_sel, batch + 1)
                pe.wait_ge(s_early_msg, BATCH * batch + BATCH)
                for m in range(BATCH):
                    T.matmul(ps[0:8, bass.ds(deg_cols[m], WIN)], early_deg_bank[:, slot, m, :],
                             early_hit_sel[:, slot, m, :], start=False, stop=False, skip_group_check=True)
                    T.matmul(ps[:, bass.ds(cols[m], WIN)], early_msg[:, slot, m, :], early_sel[:, slot, m, :],
                             start=False, stop=False, skip_group_check=True).then_inc(s_early_used, 1)

            def wide(layer, early_tiles=False):
                with pe.Fori(0, EARLY_PASSES if early_tiles else ITERS - FIRST_PASS[layer]) as i:
                    for k in range(U):
                        if early_tiles:
                            message = early_msg[:, 0, k % 2, :]
                            pe.wait_ge(s_early_sel, 2 * U * i + 2 * (k + 1))
                            pe.wait_ge(s_early_hit, U * i + (k + 1))
                        else:
                            message = msg[:, k, :]
                            pe.wait_ge(s_msg[k], 16 * i + 16 * (BEFORE[layer] + 1))
                            pe.wait_ge(s_sel, U * i + (U * BEFORE[layer] + k + 1))
                            if layer == 0:
                                pe.wait_ge(s_hit, U * i + (k + 1))
                        for j in range(BANKS):
                            c = slice(j * STRIDE, (j + 1) * STRIDE)
                            last = T.matmul(acc[:, j, 0:STRIDE], message, wide_sel[:, k % 2, c],
                                            start=False, stop=False, skip_group_check=True)
                            if layer == 0:
                                last = T.matmul(ps[0:8, DEG:DEG + STRIDE], bank_col[:, j, :], wide_deg[:, k % 2, c],
                                                start=False, stop=False, skip_group_check=True)
                        last.then_inc(s_early_used if early_tiles else s_used, 1)

            def spread(banks):
                pe.wait_ge(s_deg, 1)
                for d in banks:
                    if d > 0:
                        pe.wait_ge(s_deg_b, d)
                    last = T.matmul(ps[:, DEG:DEG + STRIDE], row_sel[:, d, :], deg_sb[:, 0:STRIDE],
                                    start=True, stop=(d == 0), skip_group_check=True)
                    if d > 0:
                        last = T.matmul(ps[:, DEG:DEG + WIN], row_sel[:, d - 1, :], deg_sb[:, STRIDE:BANK],
                                        start=False, stop=True, skip_group_check=True)
                    last.then_inc(s_deg_mm, 1)

            def second_steps(j):
                lo, hi = READY[j], READY[j + 1]

                def transpose_x2():
                    pe.wait_ge(s_x2, hi)
                    transposes(lambda b: x2_nm[:, b, :], lo, hi, 0).then_inc(s_x2t_mm, 1)

                def third_table():
                    pe.wait_ge(s_x2t, j + 1)
                    for b in range(lo, hi):
                        last = T.matmul(ps[:, DEG + (b - lo) * P:DEG + (b - lo + 1) * P],
                                        x2_t[:, b * P:(b + 1) * P], wtop[:, :], start=True, stop=True)
                    last.then_inc(s_tab_mm, 1)
                    for n, d in enumerate(BEGUN[j]):
                        pe.wait_ge(s_dx, sum(map(len, BEGUN[:j])) + n + 1)
                        clear(d)
                        T.matmul(acc[:, d, 0:STRIDE], wbot[:, :], deg_x[:, d, :],
                                 start=False, stop=False, skip_group_check=True)
                return transpose_x2, third_table

            def final(layer, j):
                close(j).then_inc(s_sum, 1)
                lo, hi = READY[j], READY[j + 1]
                if layer == 0:
                    if j == BANKS - 1:
                        close(BANKS, 8).then_inc(s_deg_sum, 1)
                    if j > 0:
                        pe.wait_ge(s_h_act, j + 1)
                        pe.wait_ge(s_h_dve, j)
                        for b in range(SECOND[j], SECOND[j + 1]):
                            table_product(BLOCKS + b, h_t, wall[1])
                    if j > 1:
                        root_term(1, h_t, j)
                elif layer == 1:
                    pe.wait_ge(s_z, j + 1)
                    pe.wait_ge(s_deg_b, BANKS)
                    pe.wait_ge(s_tab_sb, 2 * BLOCKS + j)
                    for b in range(lo, hi):
                        last = T.transpose(z_block(j, b), z_t[:, b * P:(b + 1) * P], ident[:, :])
                    last.then_inc(s_zn, 1)
                else:
                    pe.wait_ge(s_sig, 2 * j + 1)
                    if j > 0:
                        pe.wait_ge(s_stat2, j)
                    transposes(lambda b: z_t[:, b * P:(b + 1) * P], lo, hi, DEG).then_inc(s_sn, 1)

            def sums(layer):
                with pe.If(sorted_flag == 1):
                    at = 0
                    if layer == 0:
                        clear(BANKS, 8)
                        for j in range(EARLY_BANKS):
                            root_term(0, x_t, j)
                        for b in range(1, AHEAD):
                            early_transposes(b)
                            if b > 1:
                                early_products(b - 1, (b - 1) % 2)
                                early_sums(b - 2, b % 2)
                        with pe.Fori(0, EARLY_LOOPS) as i:
                            for half in range(2):
                                half_near(0, i, half)
                                slot = (AHEAD + half) % 2
                                early_transposes(2 * i + (AHEAD + half))
                                early_products(2 * i + (AHEAD + half - 1), 1 - slot)
                                early_sums(2 * i + (AHEAD + half - 2), slot)
                        b = EARLY_BATCHES
                        early_products(b - 1, (b - 1) % 2)
                        early_sums(b - 2, b % 2)
                        pe.wait_ge(s_early_t, b)
                        for j in range(EARLY_BANKS + BATCH, BANKS):
                            root_term(0, x_t, j)
                        early_sums(b - 1, (b - 1) % 2)
                        root_term(0, x_t, EARLY_BANKS)
                        half_near(0, EARLY_LOOPS, 0)
                        half_near(0, EARLY_LOOPS, 1)
                        for j in range(EARLY_BANKS + 1, EARLY_BANKS + BATCH):
                            root_term(0, x_t, j)
                        at = EARLY_END + 1
                    for passes, what, arg in stops(layer):
                        if passes > at:
                            near(layer, at, passes)
                            at = passes
                        final(layer, arg) if what == "final" else spread(arg)
                        if layer == 1 and what == "final":
                            for half, step in enumerate(second_steps(arg)):
                                if passes < ITERS:
                                    if passes < ITERS - 1 or half == 0:
                                        half_near(1, passes, half)
                                    at = passes + 1
                                step()
                            if passes == ITERS - 1:
                                half_near(1, passes, 1)
                with pe.Else():
                    if layer == 0:
                        for b in range(1, EARLY_BATCHES):
                            early_transposes(b)
                            early_products(b, b % 2)
                        pe.wait_ge(s_early_msg, EARLY)
                        clear(BANKS, 8)
                        for j in range(BANKS):
                            root_term(0, x_t, j)
                        wide(0, early_tiles=True)
                    wide(layer)
                    for _, what, arg in stops(layer):
                        final(layer, arg) if what == "final" else spread(arg)
                        if layer == 1 and what == "final":
                            for step in second_steps(arg):
                                step()

            pe.wait_ge(s_tab_sb, FIRST_PIECE[1])
            sums(0)
            pe.wait_ge(s_tab_sb, FIRST_PIECE[2])
            for j in range(2):
                root_term(1, h_t, j)
            sums(1)
            sums(2)


def edges_by_tile(a):
    return np.ascontiguousarray(np.pad(np.asarray(a), (0, TILES * P - N_EDGES), mode="edge").reshape(TILES, P).T)


def kernel(x, src, dst, edge_type_4, edge_weight, L0_gnn_W1, L0_gnn_root1, L0_gnn_b1, L0_gnn_W2, L0_gnn_root2,
           L0_gnn_b2, L1_gnn_W, L1_gnn_b):
    import concourse.bacc as bacc
    from concourse.bass_utils import run_bass_kernel_spmd

    laid = {
        "x": np.pad(np.asarray(x), ((0, NP - N_NODES), (0, 0))).T,
        "x_rows": x,
        "src": edges_by_tile(src), "dst": edges_by_tile(dst),
        "types": edges_by_tile(edge_type_4), "weights": edges_by_tile(edge_weight),
        "w1": L0_gnn_W1, "root1": L0_gnn_root1, "b1": L0_gnn_b1,
        "w2": L0_gnn_W2, "root2": L0_gnn_root2, "b2": L0_gnn_b2, "w3": L1_gnn_W, "b3": L1_gnn_b,
    }
    nc = bacc.Bacc("TRN2", target_bir_lowering=False, num_devices=1)
    arrays, args = {}, []
    for name, a in laid.items():
        a = np.ascontiguousarray(a)
        arrays[f"in_{name}"] = a
        args.append(nc.dram_tensor(f"in_{name}", a.shape, mybir.dt.from_np(a.dtype), kind="ExternalInput").ap())
    args.append(nc.dram_tensor("out_y", (N_NODES, FEAT), mybir.dt.float32, kind="ExternalOutput").ap())
    build(nc, *args)
    r = run_bass_kernel_spmd(nc, [arrays], core_ids=[0])
    return r.results[0]["out_y"]
```

```python
import numpy as np
import concourse.bass as bass
from concourse import mybir
from contextlib import ExitStack

N_NODES, FEAT, N_EDGES, RELS = 3125, 128, 50000, 4
P = 128
BLOCKS = -(-N_NODES // P)
NP = BLOCKS * P
TILES = -(-N_EDGES // P)
LAST_EDGES = N_EDGES - (TILES - 1) * P
U = 17
ITERS = TILES // U
HALVES = [(0, 9), (9, U)]
assert ITERS * U == TILES
EARLY_PASSES = 2
EARLY = U * EARLY_PASSES
BATCH = 2
EARLY_BATCHES = EARLY // BATCH
AHEAD = 5
EARLY_LOOPS = (EARLY_BATCHES - AHEAD) // 2
EARLY_END = EARLY_PASSES + EARLY_LOOPS
FIRST_PASS = [EARLY_PASSES, 0, 0]
BEFORE = [0, ITERS - EARLY_PASSES, 2 * ITERS - EARLY_PASSES]
assert EARLY == BATCH * (AHEAD + 2 * EARLY_LOOPS)
BANK = 512
WIN = 64
STRIDE = BANK - WIN
BANKS = -(-N_NODES // STRIDE)
DEG = BANKS * BANK
ALLN = BANKS * STRIDE
PARTS = [(j, 0, STRIDE) for j in range(BANKS - 1)] + [(BANKS - 1, 0, 2 * P), (BANKS - 1, 2 * P, STRIDE)]
LAST_HALF = len(PARTS) - 2
READY = [(bank * STRIDE + first) // P for bank, first, _ in PARTS] + [BLOCKS]
FINAL = [18, 26, 32, 36, 40, 44, 45, 2 * ITERS]
SECOND = [0, 0, 4, 9, 13, 17, 21, 23, BLOCKS]
SPREAD = [(6, range(0, 4)), (12, range(4, BANKS))]
BEGUN = [[], [], [1], [2], [3], [], [], [4, 5, 6, 0]]
assert len(FINAL) == len(BEGUN) == len(PARTS) and max(b - a for a, b in zip(READY, READY[1:])) <= 4
assert all(s <= r for s, r in zip(SECOND, READY))
FIRST_BATCH = 20
STAGES = 4
EARLY_BANKS = 3
BEGIN = [(EARLY_END, EARLY_BANKS), (EARLY_END + 1, EARLY_BANKS + 1)]
assert EARLY_BANKS + BATCH + 1 < BANKS and 2 * EARLY_END < FINAL[0]
X_PARTS = [(0, 4 * P), (4 * P, 12 * P), (12 * P, NP)]
EPS = 1e-5


def build(nc, x, x_rows, srcs, dsts, types, weights, w1, root1, b1, w2, root2, b2, w3, b3, out):
    fp32, bf16, i32 = mybir.dt.float32, mybir.dt.bfloat16, mybir.dt.int32
    ALU, ACT, AX = mybir.AluOpType, mybir.ActivationFunctionType, mybir.AxisListType

    tables = [nc.dram_tensor(f"table{n}", (NP, RELS * FEAT if n < 2 else FEAT), fp32, kind="Internal").ap()
              for n in range(3)]
    rows = [t.rearrange("n (r f) -> (n r) f", f=FEAT) for t in tables[:2]] + [tables[2]]

    with ExitStack() as ctx:
        def sb(name, shape, dt=fp32):
            return ctx.enter_context(nc.sbuf_tensor(name, shape, dt))

        def sem(name):
            return ctx.enter_context(nc.semaphore(name))

        src_i = sb("src_i", [P, TILES], i32)
        dst_i = sb("dst_i", [P, TILES], i32)
        typ_i = sb("typ_i", [P, TILES], i32)
        ew = sb("ew", [P, TILES])
        wall = [sb(f"wall{n}", [P, RELS, FEAT]) for n in range(2)]
        root = [sb(f"root{n}", [P, FEAT]) for n in range(2)]
        bias = [sb(f"bias{n}", [P, 1]) for n in range(2)]
        wtop = sb("wtop", [P, FEAT])
        wbot = sb("wbot", [P, FEAT])
        b3_all = sb("b3_all", [P, FEAT])
        iota = sb("iota", [P, ALLN])
        part = sb("part", [P, 1])
        ident = sb("ident", [P, P])
        ones_row = sb("ones_row", [1, P])
        zeros = sb("zeros", [P, BANK], bf16)
        row_sel = sb("row_sel", [8, BANKS, P])
        bank_col = sb("bank_col", [P, BANKS, 8], bf16)
        eps = sb("eps", [P, 1])
        dst_f = sb("dst_f", [P, TILES])
        base_f = sb("base_f", [P, TILES])
        rel_f = sb("rel_f", [P, TILES])
        bank_f = sb("bank_f", [P, TILES])
        idx12 = sb("idx12", [P, TILES], i32)
        w12 = sb("w12", [P, TILES])
        real = sb("real", [P, 1])
        col_i = sb("col_i", [1, TILES], i32)
        deg_col_i = sb("deg_col_i", [1, TILES], i32)
        col_t = sb("col_t", [1, TILES])
        ext = sb("ext", [P, 4])
        outside = sb("outside", [P, len(PARTS) + len(BEGIN)])
        is_type = sb("is_type", [P, RELS, EARLY])
        ext_all = sb("ext_all", [P, 4])
        scale2 = sb("scale2", [P, 2])
        ok_f = sb("ok_f", [1, 2])
        ok_i = sb("ok_i", [1, 1], i32)
        idx_slot = sb("idx_slot", [P, U], i32)
        msg = sb("msg", [P, U, FEAT])
        sel = sb("sel", [P, U, WIN])
        hit_sel = sb("hit_sel", [P, U, WIN], bf16)
        deg_bank = sb("deg_bank", [P, U, 8], bf16)
        wide_sel = sb("wide_sel", [P, 2, ALLN])
        wide_deg = sb("wide_deg", [P, 2, ALLN], bf16)
        early_t = sb("early_t", [P, 2, BATCH * P])
        early_now = sb("early_now", [P, BATCH, FEAT])
        early_msg = sb("early_msg", [P, 2, BATCH, FEAT])
        early_sel = sb("early_sel", [P, 2, BATCH, WIN])
        early_hit_sel = sb("early_hit_sel", [P, 2, BATCH, WIN], bf16)
        early_deg_bank = sb("early_deg_bank", [P, 2, BATCH, 8], bf16)
        stage = sb("stage", [P, STAGES, BANK])
        x_t = sb("x_t", [P, NP])
        h_t = sb("h_t", [P, NP])
        z_t = sb("z_t", [P, NP])
        node_rows = sb("node_rows", [P, 2 * BLOCKS, FEAT])
        x2_nm = node_rows[:, 0:BLOCKS, :]
        u_nm = node_rows[:, BLOCKS:2 * BLOCKS, :]
        early = node_rows[:, 0:EARLY, :]
        x2_t = sb("x2_t", [P, NP])
        deg_sb = sb("deg_sb", [8, BANK])
        deg_x = sb("deg_x", [P, BANKS, STRIDE])
        shared = sb("shared", [P, BANKS - 1, WIN])
        shared2 = sb("shared2", [P, BANKS - 1, WIN])
        stats = sb("stats", [P, BLOCKS, 6])
        mv = sb("mv", [P, BLOCKS, 2])
        rstd = sb("rstd", [P, BLOCKS])
        nmr = sb("nmr", [P, BLOCKS])

        ps = ctx.enter_context(nc.psum_tensor("ps", [P, 8 * BANK], fp32))
        acc = ps[:, 0:BANKS * BANK].rearrange("p (j c) -> p j c", c=BANK)

        s_ld_x = [sem(f"s_ld_x{n}") for n in range(len(X_PARTS))]
        s_ld_w1, s_ld_dst, s_ld_e, s_ld_w = sem("s_ld_w1"), sem("s_ld_dst"), sem("s_ld_e"), sem("s_ld_w")
        s_ld_src = sem("s_ld_src")
        s_clear, s_const, s_order = sem("s_clear"), sem("s_const"), sem("s_order")
        s_wide_iota = sem("s_wide_iota")
        s_early_now, s_early_part = sem("s_early_now"), sem("s_early_part")
        s_early_ahead, s_early_rest = sem("s_early_ahead"), sem("s_early_rest")
        s_early_tr, s_early_t, s_early_mm, s_early_msg = (
            sem("s_early_tr"), sem("s_early_t"), sem("s_early_mm"), sem("s_early_msg"))
        s_early_hit, s_early_sel, s_early_used = sem("s_early_hit"), sem("s_early_sel"), sem("s_early_used")
        s_dstf, s_base_mm, s_ext, s_ext_all, s_edges = (
            sem("s_dstf"), sem("s_base_mm"), sem("s_ext"), sem("s_ext_all"), sem("s_edges"))
        s_tab_mm, s_tab_sb = sem("s_tab_mm"), sem("s_tab_sb")
        s_tab_out = [sem(f"s_tab_out{n}") for n in range(STAGES)]
        s_idx, s_gate = sem("s_idx"), sem("s_gate")
        s_msg = [sem(f"s_msg{k}") for k in range(U)]
        s_hit, s_sel, s_used = sem("s_hit"), sem("s_sel"), sem("s_used")
        s_sum, s_deg_sum = sem("s_sum"), sem("s_deg_sum")
        s_deg, s_deg_mm, s_deg_b = sem("s_deg"), sem("s_deg_mm"), sem("s_deg_b")
        s_bank_read = sem("s_bank_read")
        s_h_act, s_h_dve = sem("s_h_act"), sem("s_h_dve")
        s_z, s_zn, s_stat, s_std, s_rstd, s_x2 = (
            sem("s_z"), sem("s_zn"), sem("s_stat"), sem("s_std"), sem("s_rstd"), sem("s_x2"))
        s_x2t_mm, s_x2t, s_dx, s_sp = sem("s_x2t_mm"), sem("s_x2t"), sem("s_dx"), sem("s_sp")
        s_ov, s_sig, s_sn, s_stat2, s_std2, s_rstd2, s_y, s_out = (
            sem("s_ov"), sem("s_sig"), sem("s_sn"), sem("s_stat2"), sem("s_std2"), sem("s_rstd2"),
            sem("s_y"), sem("s_out"))
        block = ctx.enter_context(nc.Block())

        def stops(layer):
            found = [(p, "final", j) for j, p in enumerate(FINAL)]
            return sorted(found + [(p, "spread", banks) for p, banks in SPREAD] * (layer == 1), key=lambda s: s[0])

        FIRST_PIECE = [0, BLOCKS, 2 * BLOCKS, 2 * BLOCKS + len(PARTS)]
        def table_done(layer, slot):
            return 16 * len([n for n in range(FIRST_PIECE[layer + 1]) if n % STAGES == slot])

        def shared_norm(lo, hi):
            return lo + (hi - lo + 1) // 2

        def z_block(j, b):
            lo, mid = READY[j], shared_norm(READY[j], READY[j + 1])
            column = DEG + (b - lo) * P if b < mid else (b - mid) * P
            return ps[:, column:column + P]

        @block.sync
        def _(sp):
            sp.dma_start(wall[0][:, :, :], w1.rearrange("r i o -> i r o")).then_inc(s_ld_w1, 16)
            for n, (lo, hi) in enumerate(X_PARTS):
                sp.dma_start(x_t[:, lo:hi], x[:, lo:hi]).then_inc(s_ld_x[n], 16)
                if n == 0:
                    sp.dma_start(dst_i[:, :], dsts).then_inc(s_ld_dst, 16)
            sp.dma_start(root[0][:, :], root1).then_inc(s_ld_w, 16)
            sp.dma_start(bias[0][:, :], b1.rearrange("(f a) -> f a", a=1)).then_inc(s_ld_w, 16)
            sp.dma_start(wall[1][:, :, :], w2.rearrange("r i o -> i r o")).then_inc(s_ld_w, 16)
            sp.dma_start(root[1][:, :], root2).then_inc(s_ld_w, 16)
            sp.dma_start(bias[1][:, :], b2.rearrange("(f a) -> f a", a=1)).then_inc(s_ld_w, 16)
            sp.dma_start(wtop[:, :], w3[0:FEAT, :]).then_inc(s_ld_w, 16)
            sp.dma_start(wbot[:, :], w3[FEAT:2 * FEAT, :]).then_inc(s_ld_w, 16)
            sp.dma_start(b3_all[:, :], b3.rearrange("(a f) -> a f", a=1).to_broadcast([P, FEAT])).then_inc(s_ld_w, 16)
            for layer in range(3):
                for n in range(FIRST_PIECE[layer], FIRST_PIECE[layer + 1]):
                    sp.wait_ge(s_tab_sb, n + 1)
                    b = n - FIRST_PIECE[layer]
                    if layer < 2:
                        dest, piece = tables[layer][b * P:(b + 1) * P, :], stage[:, n % STAGES, :]
                    else:
                        dest = tables[2][READY[b] * P:READY[b + 1] * P, :].rearrange("(q p) f -> p q f", p=P)
                        piece = stage[:, n % STAGES, 0:(READY[b + 1] - READY[b]) * FEAT]\
                            .rearrange("p (q f) -> p q f", f=FEAT)
                    sp.dma_start(dest, piece).then_inc(s_tab_out[n % STAGES], 16)
            count = 0
            for j in range(len(PARTS)):
                sp.wait_ge(s_y, READY[j + 1])
                lo, hi = READY[j], min(READY[j + 1], N_NODES // P)
                sp.dma_start(out[lo * P:hi * P, :].rearrange("(b p) f -> p b f", p=P),
                             x2_nm[:, lo:hi, :]).then_inc(s_out, 16)
                count += 1
            sp.dma_start(out[(BLOCKS - 1) * P:N_NODES, :],
                         x2_nm[0:N_NODES - (BLOCKS - 1) * P, BLOCKS - 1, :]).then_inc(s_out, 16)
            count += 1
            sp.wait_ge(s_out, 16 * count)

        @block.gpsimd
        def _(pool):
            nc.gpsimd.memset(ident[:, :], 0.0).then_inc(s_clear, 1)
            nc.gpsimd.memset(row_sel[:, :, :], 0.0).then_inc(s_clear, 1)
            nc.gpsimd.iota(iota[:, 0:WIN], [[1, WIN]], base=0, channel_multiplier=0,
                           allow_small_or_imprecise_dtypes=True).then_inc(s_const, 1)
            nc.gpsimd.iota(part[:, :], [[0, 1]], base=0, channel_multiplier=1,
                           allow_small_or_imprecise_dtypes=True).then_inc(s_const, 1)
            pool.wait_ge(s_clear, 2)
            nc.gpsimd.affine_select(out=ident[:, :], in_=ident[:, :], compare_op=ALU.not_equal, fill=1.0,
                                    base=0, pattern=[[-1, P]], channel_multiplier=1).then_inc(s_const, 1)
            nc.gpsimd.affine_select(out=row_sel[:, :, :], in_=row_sel[:, :, :], compare_op=ALU.not_equal,
                                    fill=1.0, base=0, pattern=[[-1, BANKS], [0, P]],
                                    channel_multiplier=1).then_inc(s_const, 1)
            def early_rows(lo, hi, done):
                for t in range(lo, hi):
                    pool.indirect_dma_start(early[:, t, :], None, x_rows,
                                            bass.IndirectOffsetOnAxis(src_i[:, t:t + 1], 0)).then_inc(done, 16)

            pool.wait_ge(s_ld_src, 16)
            early_rows(0, AHEAD * BATCH, s_early_ahead)
            early_rows(AHEAD * BATCH, U, s_early_rest)
            pool.wait_ge(s_ext, 4)
            nc.gpsimd.partition_all_reduce(ext_all[:, :], ext[:, :], P, bass.bass_isa.ReduceOp.max)\
                .then_inc(s_ext_all, 1)
            early_rows(U, EARLY, s_early_rest)
            for layer in range(3):
                for n in range(STAGES):
                    pool.wait_ge(s_tab_out[n], table_done(layer, n))
                with pool.Fori(0, ITERS - FIRST_PASS[layer]) as i:
                    for half, (lo, hi) in enumerate(HALVES):
                        pool.wait_ge(s_idx, 2 * i + (2 * BEFORE[layer] + half + 1))
                        pool.sem_inc(s_gate, 1)
                        for k in range(lo, hi):
                            pool.indirect_dma_start(
                                msg[:, k, :], None, rows[layer],
                                bass.IndirectOffsetOnAxis(idx_slot[:, k:k + 1], 0)).then_inc(s_msg[k], 16)

        @block.scalar
        def _(act):
            act.dma_start(src_i[:, :], srcs).then_inc(s_ld_src, 16)
            act.dma_start(typ_i[:, :], types).then_inc(s_ld_e, 16)
            act.dma_start(ew[:, :], weights).then_inc(s_ld_e, 16)

            def table_piece(n):
                bank = n % 2
                act.wait_ge(s_tab_mm, n + 1)
                if n >= STAGES:
                    act.wait_ge(s_tab_out[n % STAGES], 16 * (n // STAGES))
                nc.scalar.copy(stage[:, n % STAGES, :], ps[:, bank * BANK:(bank + 1) * BANK])\
                    .then_inc(s_tab_sb, 1)

            def half_indices(layer, i, lo, hi):
                table = idx12 if layer < 2 else src_i
                act.wait_ge(s_used, U * i + (U * BEFORE[layer] + hi))
                nc.scalar.copy(idx_slot[:, lo:hi], table[:, bass.ds(U * i + (U * FIRST_PASS[layer] + lo), hi - lo)])\
                    .then_inc(s_idx, 1)

            def indices(layer, start, end):
                with act.Fori(start - FIRST_PASS[layer], end - FIRST_PASS[layer]) as i:
                    for lo, hi in HALVES:
                        half_indices(layer, i, lo, hi)

            def early_batch(batch, slot):
                early_rows(batch)
                early_transposed(batch, slot)

            def early_rows(batch):
                nc.scalar.copy(early_now[:, :, :], early[:, bass.ds(batch * BATCH, BATCH), :]).then_inc(s_early_now, 1)

            def early_transposed(batch, slot):
                act.wait_ge(s_early_tr, batch + 1)
                nc.scalar.copy(early_t[:, slot, :], acc[:, BANKS - 1, 0:BATCH * P]).then_inc(s_early_t, 1)

            for n in range(BLOCKS):
                if n == FIRST_BATCH - 1:
                    act.wait_ge(s_early_ahead, 16 * AHEAD * BATCH)
                    early_rows(0)
                elif n == FIRST_BATCH:
                    early_transposed(0, 0)
                table_piece(n)

            def softplus():
                act.wait_ge(s_x2, BLOCKS)
                nc.scalar.activation(u_nm[:, :, :], x2_nm[:, :, :], ACT.Exp).then_inc(s_sp, 1)
                act.wait_ge(s_sp, 1)
                nc.scalar.activation(u_nm[:, :, :], u_nm[:, :, :], ACT.Ln, bias=1.0).then_inc(s_sp, 1)

            def norm(j, stat, std, ready, source, done):
                lo, hi = READY[j], READY[j + 1]
                act.wait_ge(stat, j + 1)
                nc.scalar.activation(rstd[:, lo:hi], mv[:, lo:hi, 1], ACT.Sqrt, bias=eps[:, 0:1]).then_inc(std, 1)
                act.wait_ge(ready, j + 1)
                for b in range(lo, shared_norm(lo, hi)):
                    nc.scalar.activation(x2_nm[:, b, :], source(b), ACT.Identity,
                                         bias=nmr[:, b:b + 1], scale=rstd[:, b:b + 1]).then_inc(done, 1)

            def final(layer, j):
                bank, first, end = PARTS[j]
                lo = WIN if first == 0 and bank > 0 else first
                if first > 0:
                    act.wait_ge(s_sum, len(PARTS) * layer + j + 1)
                if layer == 0:
                    act.wait_ge(s_bank_read, bank + 1)
                    nc.scalar.activation(h_t[:, bank * STRIDE + lo:bank * STRIDE + end], acc[:, bank, lo:end],
                                         ACT.Relu, bias=bias[0][:, 0:1]).then_inc(s_h_act, 1)
                    for b in range(SECOND[j], SECOND[j + 1]):
                        table_piece(BLOCKS + b)
                elif layer == 1:
                    norm(j, s_stat, s_std, s_rstd, lambda b: z_block(j, b), s_x2)
                else:
                    act.wait_ge(s_ov, bank + 1)
                    if first == 0 and bank > 0:
                        nc.scalar.activation(z_t[:, bank * STRIDE:bank * STRIDE + WIN], shared2[:, bank - 1, :],
                                             ACT.Sigmoid).then_inc(s_sig, 1)
                    nc.scalar.activation(z_t[:, bank * STRIDE + lo:bank * STRIDE + end], acc[:, bank, lo:end],
                                         ACT.Sigmoid).then_inc(s_sig, 1)
                    norm(j, s_stat2, s_std2, s_rstd2, lambda b: u_nm[:, b, :], s_y)

            def spread(banks):
                for d in banks:
                    act.wait_ge(s_deg_mm, d + 1)
                    nc.scalar.copy(deg_x[:, d, :], ps[:, DEG:DEG + STRIDE]).then_inc(s_deg_b, 1)

            act.wait_ge(s_edges, 3)
            sorted_flag = act.value_load(ok_i[0:1, 0:1], min_val=0, max_val=1)
            for layer in range(3):
                if layer == 0:
                    indices(0, EARLY_PASSES, EARLY_PASSES + 1)
                with act.If(sorted_flag == 1):
                    at = 0
                    if layer == 0:
                        for b in range(1, AHEAD):
                            early_batch(b, b % 2)
                        act.wait_ge(s_early_rest, 16 * (EARLY - AHEAD * BATCH))
                        with act.Fori(0, EARLY_LOOPS) as i:
                            for half, (lo, hi) in enumerate(HALVES):
                                half_indices(0, i + 1, lo, hi)
                                early_batch(2 * i + (AHEAD + half), (AHEAD + half) % 2)
                        at = EARLY_END + 1
                    if layer == 2:
                        indices(2, 0, 2)
                        softplus()
                        at = 2
                    for halves, what, arg in stops(layer):
                        to = min(halves // 2 + 1, ITERS)
                        if to > at:
                            indices(layer, at, to)
                        at = to
                        final(layer, arg) if what == "final" else spread(arg)
                with act.Else():
                    if layer == 0:
                        act.wait_ge(s_early_rest, 16 * (EARLY - AHEAD * BATCH))
                        for b in range(1, EARLY_BATCHES):
                            early_batch(b, b % 2)
                    elif layer == 2:
                        indices(2, 0, 2)
                        softplus()
                    indices(layer, [EARLY_PASSES + 1, 0, 2][layer], ITERS)
                    for _, what, arg in stops(layer):
                        final(layer, arg) if what == "final" else spread(arg)

        @block.vector
        def _(dve):
            chain = [0]

            def link(ins):
                chain[0] += 1
                ins.then_inc(s_order, 1)
                dve.wait_ge(s_order, chain[0])

            V = nc.vector
            V.memset(ones_row[:, :], 1.0).then_inc(s_const, 1)
            V.memset(zeros[:, :], 0.0).then_inc(s_const, 1)
            V.memset(eps[:, :], EPS).then_inc(s_const, 1)
            link(V.memset(bank_col[:, :, :], 0.0))
            V.memset(bank_col[:, :, :].rearrange("p a b -> p (a b)")[:, 0:8 * BANKS:9], 1.0).then_inc(s_const, 1)
            V.memset(h_t[:, ALLN:NP], 0.0).then_inc(s_const, 1)
            V.memset(z_t[:, ALLN:NP], 0.0).then_inc(s_const, 1)
            dve.wait_ge(s_ld_dst, 16)
            V.tensor_copy(dst_f[:, :], dst_i[:, :]).then_inc(s_dstf, 1)
            dve.wait_ge(s_ld_src, 16)
            dve.wait_ge(s_ld_e, 32)
            link(V.scalar_tensor_tensor(idx12[:, :], src_i[:, :], float(RELS), typ_i[:, :], ALU.mult, ALU.add))
            V.reduce_max(ext[:, 0:1], ew[:, :], axis=AX.X).then_inc(s_ext, 1)
            V.tensor_reduce(ext[:, 1:2], ew[:, :], AX.X, ALU.min, negate=True).then_inc(s_ext, 1)
            dve.wait_ge(s_base_mm, 1)
            link(V.tensor_copy(base_f[:, :], ps[:, DEG:DEG + TILES]))
            link(V.tensor_tensor(rel_f[:, :], dst_f[:, :], base_f[:, :], ALU.subtract))
            V.reduce_max(ext[:, 2:3], rel_f[:, :], axis=AX.X).then_inc(s_ext, 1)
            link(V.tensor_reduce(outside[:, len(PARTS) - 1:len(PARTS)], rel_f[:, :], AX.X, ALU.min, negate=True))
            for j, (bank, _, end) in enumerate(PARTS[:-1]):
                after = U * (FINAL[j] // 2) + HALVES[FINAL[j] % 2][0]
                link(V.tensor_reduce(outside[:, j:j + 1], dst_f[:, after:TILES], AX.X, ALU.min, negate=True))
                link(V.tensor_scalar_add(outside[:, j:j + 1], outside[:, j:j + 1], float(STRIDE * bank + end)))
            for n, (passes, banks) in enumerate(BEGIN):
                above = outside[:, len(PARTS) + n:len(PARTS) + n + 1]
                link(V.reduce_max(above, dst_f[:, 0:U * passes], axis=AX.X))
                link(V.tensor_scalar_add(above, above, float(1 - STRIDE * banks)))
            V.reduce_max(ext[:, 3:4], outside[:, :], axis=AX.X).then_inc(s_ext, 1)
            for r in range(RELS):
                V.tensor_single_scalar(is_type[:, r, :], typ_i[:, 0:EARLY], float(r), ALU.is_equal)\
                    .then_inc(s_order, 1)
                chain[0] += 1
            link(V.tensor_single_scalar(bank_f[:, :], base_f[:, :], float(STRIDE), ALU.is_ge))
            for j in range(2, BANKS):
                link(V.scalar_tensor_tensor(bank_f[:, :], base_f[:, :], float(STRIDE * j), bank_f[:, :],
                                            ALU.is_ge, ALU.add))
            V.scalar_tensor_tensor(col_i[:, :], bank_f[0:1, :], float(WIN), base_f[0:1, :], ALU.mult, ALU.add)\
                .then_inc(s_edges, 1)
            link(V.scalar_tensor_tensor(col_t[:, :], bank_f[0:1, :], -float(STRIDE), base_f[0:1, :],
                                        ALU.mult, ALU.add))
            V.tensor_scalar_add(deg_col_i[:, :], col_t[:, :], float(DEG)).then_inc(s_edges, 1)
            dve.wait_ge(s_const, 10)
            link(V.tensor_single_scalar(real[:, :], part[:, :], float(LAST_EDGES), ALU.is_lt))
            for dest in (rel_f, dst_f):
                link(V.scalar_tensor_tensor(dest[:, TILES - 1:TILES], dest[:, TILES - 1:TILES], 1.0, real[:, :],
                                            ALU.add, ALU.mult))
                link(V.tensor_scalar_add(dest[:, TILES - 1:TILES], dest[:, TILES - 1:TILES], -1.0))
            dve.wait_ge(s_ext_all, 1)
            link(V.tensor_tensor(scale2[:, 0:1], ext_all[:, 0:1], ext_all[:, 1:2], ALU.add))
            link(V.tensor_scalar_add(scale2[:, 0:1], scale2[:, 0:1], 1e-8))
            link(V.reciprocal(scale2[:, 1:2], scale2[:, 0:1]))
            link(V.tensor_scalar(w12[:, :], ew[:, :], ext_all[:, 1:2], scale2[:, 1:2], ALU.add, ALU.mult))
            link(V.tensor_single_scalar(ok_f[:, 0:1], ext_all[0:1, 2:3], float(WIN), ALU.is_lt))
            link(V.tensor_single_scalar(ok_f[:, 1:2], ext_all[0:1, 3:4], 0.0, ALU.is_le))
            link(V.tensor_tensor(ok_i[:, :], ok_f[:, 0:1], ok_f[:, 1:2], ALU.mult))
            dve.wait_ge(s_ld_w, 128)
            V.engine_nop().then_inc(s_edges, 1)
            sorted_flag = dve.value_load(ok_i[0:1, 0:1], min_val=0, max_val=1)

            def select(layer, t, n, sel_to, hit_to, bank_to, hit, hits, done):
                tiles, wide = bass.ds(t, n), [P, n, WIN]
                columns = iota[:, 0:WIN].unsqueeze(1).to_broadcast(wide)
                rel = rel_f[:, tiles].unsqueeze(2).to_broadcast(wide)
                if layer == 2:
                    V.tensor_tensor(sel_to, columns, rel, ALU.is_equal).then_inc(done, 1)
                    return
                V.tensor_tensor(hit_to, columns, rel, ALU.is_equal).then_inc(hit, 1)
                if layer == 0:
                    V.tensor_tensor(bank_to, iota[:, 0:8].unsqueeze(1).to_broadcast([P, n, 8]),
                                    bank_f[:, tiles].unsqueeze(2).to_broadcast([P, n, 8]), ALU.is_equal)\
                        .then_inc(hit, 1)
                dve.wait_ge(hit, hits)
                V.tensor_tensor(sel_to, hit_to, w12[:, tiles].unsqueeze(2).to_broadcast(wide), ALU.mult)\
                    .then_inc(done, 1)

            def half_near(layer, i, half):
                lo, hi = HALVES[half]
                dve.wait_ge(s_used, U * i + (U * BEFORE[layer] + hi))
                hits = 4 * i + 2 * (half + 1) if layer == 0 else 2 * i + (4 * BEFORE[1] + half + 1)
                select(layer, U * i + (U * FIRST_PASS[layer] + lo), hi - lo, sel[:, lo:hi, :], hit_sel[:, lo:hi, :],
                       deg_bank[:, lo:hi, :], s_hit, hits, s_sel)

            def near(layer, start, end):
                with dve.Fori(start - FIRST_PASS[layer], end - FIRST_PASS[layer]) as i:
                    for half in range(2):
                        half_near(layer, i, half)

            def early_place(batch, m):
                return early[:, bass.ds(batch * BATCH + m, 1), :].rearrange("p a f -> p (a f)")

            def early_messages(batch, place):
                for m in range(BATCH):
                    dve.wait_ge(s_early_mm, BATCH * batch + (m + 1))
                    for r in range(RELS):
                        holds = is_type[:, r, bass.ds(batch * BATCH + m, 1)]
                        product = acc[:, EARLY_BANKS + m, r * FEAT:(r + 1) * FEAT]
                        if r == 0:
                            last = V.tensor_scalar(place(batch, m), product, holds, None, ALU.mult)
                        else:
                            dve.wait_ge(s_early_part, (RELS - 1) * BATCH * batch + ((RELS - 1) * m + r))
                            last = V.scalar_tensor_tensor(place(batch, m), product, holds, place(batch, m),
                                                          ALU.mult, ALU.add)
                        last.then_inc(s_early_msg if r == RELS - 1 else s_early_part, 1)

            def early_near(batch, slot):
                dve.wait_ge(s_early_used, BATCH * batch + (U - BATCH))
                select(0, batch * BATCH, BATCH, early_sel[:, slot, :, :], early_hit_sel[:, slot, :, :],
                       early_deg_bank[:, slot, :, :], s_early_hit, 2 * batch + 2, s_early_sel)
                early_messages(batch, lambda batch, m: early_msg[:, slot, m, :])

            def wide(layer, early_tiles=False):
                first = 0 if early_tiles else U * FIRST_PASS[layer]
                before = 0 if early_tiles else U * BEFORE[layer]
                used = s_early_used if early_tiles else s_used
                with dve.Fori(0, EARLY_PASSES if early_tiles else ITERS - FIRST_PASS[layer]) as i:
                    for k in range(U):
                        done = k if k == 0 else k - 1
                        dve.wait_ge(used, U * i + (before + U + done))
                        if early_tiles:
                            V.tensor_copy(early_msg[:, 0, k % 2, :].unsqueeze(1), early[:, bass.ds(U * i + k, 1), :])\
                                .then_inc(s_early_sel, 1)
                        dst = dst_f[:, bass.ds(U * i + (first + k), 1)]
                        if layer == 2:
                            V.tensor_scalar(wide_sel[:, k % 2, :], iota[:, :], dst, None, ALU.is_equal)\
                                .then_inc(s_sel, 1)
                        else:
                            V.tensor_scalar(wide_sel[:, k % 2, :], iota[:, :], dst,
                                            w12[:, bass.ds(U * i + (first + k), 1)], ALU.is_equal, ALU.mult)\
                                .then_inc(s_early_sel if early_tiles else s_sel, 1)
                        if layer == 0:
                            V.tensor_scalar(wide_deg[:, k % 2, :], iota[:, :], dst, None, ALU.is_equal)\
                                .then_inc(s_early_hit if early_tiles else s_hit, 1)

            def statistics(j, source, done):
                lo, hi = READY[j], READY[j + 1]
                for b in range(lo, hi):
                    last = V.bn_stats(stats[:, b, :], source(b))
                    if b < hi - 1:
                        last.then_inc(s_order, 1)
                        chain[0] += 1
                link(last)
                for b in range(lo, hi):
                    last = V.bn_aggr(mv[:, b, :], stats[:, b, :])
                    if b < hi - 1:
                        last.then_inc(s_order, 1)
                        chain[0] += 1
                last.then_inc(done, 1)

            def norm(j, std, ready, source, done):
                lo, hi = READY[j], READY[j + 1]
                dve.wait_ge(std, j + 1)
                link(V.reciprocal(rstd[:, lo:hi], rstd[:, lo:hi]))
                V.scalar_tensor_tensor(nmr[:, lo:hi], mv[:, lo:hi, 0], -1.0, rstd[:, lo:hi],
                                       ALU.mult, ALU.mult).then_inc(ready, 1)
                dve.wait_ge(ready, j + 1)
                for b in range(shared_norm(lo, hi), hi):
                    V.tensor_scalar(x2_nm[:, b, :], source(b), rstd[:, b:b + 1], nmr[:, b:b + 1], ALU.mult, ALU.add)\
                        .then_inc(done, 1)

            def final(layer, j):
                dve.wait_ge(s_sum, len(PARTS) * layer + j + 1)
                bank, begin, end = PARTS[j]
                has_first, has_common = begin == 0 and bank > 0, end == STRIDE and bank < BANKS - 1
                nodes = slice(bank * STRIDE + begin, bank * STRIDE + end)
                first = slice(bank * STRIDE, bank * STRIDE + WIN)
                common = acc[:, bank, STRIDE:BANK]
                if layer == 0:
                    if has_common:
                        last = V.tensor_scalar(shared[:, bank, :], common, bias[0][:, 0:1], None, ALU.add)
                        if j == 0:
                            last.then_inc(s_bank_read, 1)
                            dve.wait_ge(s_bank_read, 1)
                        else:
                            link(last)
                    if has_first:
                        V.tensor_tensor(shared2[:, bank - 1, :], acc[:, bank, 0:WIN], shared[:, bank - 1, :], ALU.add)\
                            .then_inc(s_bank_read, 1)
                        dve.wait_ge(s_bank_read, bank + 1)
                        V.tensor_scalar(h_t[:, first], shared2[:, bank - 1, :], 0.0, None, ALU.max).then_inc(s_h_dve, 1)
                elif layer == 1:
                    if has_common:
                        link(V.tensor_copy(shared[:, bank, :], common))
                    last = V.scalar_tensor_tensor(z_t[:, nodes], acc[:, bank, begin:end], bias[1][:, 0:1],
                                                  x_t[:, nodes], ALU.add, ALU.add)
                    if has_first:
                        link(last)
                        last = V.tensor_tensor(z_t[:, first], z_t[:, first], shared[:, bank - 1, :], ALU.add)
                    last.then_inc(s_z, 1)
                    dve.wait_ge(s_zn, j + 1)
                    statistics(j, lambda b: z_block(j, b), s_stat)
                    norm(j, s_std, s_rstd, lambda b: z_block(j, b), s_x2)
                    dve.wait_ge(s_x2t_mm, j + 1)
                    V.tensor_copy(x2_t[:, READY[j] * P:READY[j + 1] * P], ps[:, 0:(READY[j + 1] - READY[j]) * P])\
                        .then_inc(s_x2t, 1)
                    n, k = 2 * BLOCKS + j, READY[j + 1] - READY[j]
                    dve.wait_ge(s_tab_mm, n + 1)
                    dve.wait_ge(s_tab_out[n % STAGES], 16 * (n // STAGES))
                    V.tensor_tensor(stage[:, n % STAGES, 0:k * FEAT].rearrange("p (q f) -> p q f", f=FEAT),
                                    ps[:, DEG:DEG + k * FEAT].rearrange("p (q f) -> p q f", f=FEAT),
                                    b3_all[:, :].unsqueeze(1).to_broadcast([P, k, FEAT]), ALU.add)\
                        .then_inc(s_tab_sb, 1)
                    for d in BEGUN[j]:
                        dve.wait_ge(s_deg_b, d + 1)
                        dve.wait_ge(s_x2t, j + 1)
                        V.tensor_tensor(deg_x[:, d, :], deg_x[:, d, :], x2_t[:, d * STRIDE:(d + 1) * STRIDE],
                                        ALU.mult).then_inc(s_dx, 1)
                else:
                    if j == 0:
                        dve.wait_ge(s_sp, 2)
                        link(V.tensor_tensor(u_nm[:, :, :], u_nm[:, :, :], x2_nm[:, :, :], ALU.add))
                    if has_common:
                        last = V.tensor_copy(shared[:, bank, :], common)
                        if j == 0:
                            last.then_inc(s_ov, 1)
                        else:
                            link(last)
                    if has_first:
                        V.tensor_tensor(shared2[:, bank - 1, :], acc[:, bank, 0:WIN], shared[:, bank - 1, :], ALU.add)\
                            .then_inc(s_ov, 1)
                    dve.wait_ge(s_sn, j + 1)
                    lo, hi = READY[j], READY[j + 1]
                    link(V.tensor_tensor(u_nm[:, lo:hi, :],
                                         ps[:, DEG:DEG + (hi - lo) * P].rearrange("p (b f) -> p b f", f=P),
                                         u_nm[:, lo:hi, :], ALU.add))
                    statistics(j, lambda b: u_nm[:, b, :], s_stat2)
                    norm(j, s_std2, s_rstd2, lambda b: u_nm[:, b, :], s_y)

            wide_iotas = 0
            for layer in range(3):
                chain_before = chain[0]
                with dve.If(sorted_flag == 1):
                    at = 0
                    if layer == 0:
                        for b in range(AHEAD - 1):
                            early_near(b, b % 2)
                        half_near(0, 0, 0)
                        with dve.Fori(0, EARLY_LOOPS) as i:
                            half_near(0, i, 1)
                            early_near(2 * i + (AHEAD - 1), (AHEAD - 1) % 2)
                            half_near(0, i + 1, 0)
                            early_near(2 * i + AHEAD, AHEAD % 2)
                        early_near(EARLY_BATCHES - 1, (EARLY_BATCHES - 1) % 2)
                        half_near(0, EARLY_LOOPS, 1)
                        at = EARLY_END + 1
                    for j in range(len(PARTS)):
                        to = min(FINAL[j] // 2 + 1, ITERS)
                        if to > at:
                            near(layer, at, to)
                        at = to
                        final(layer, j)
                with dve.Else():
                    chain[0] = chain_before
                    if layer == 0:
                        width = WIN
                        while width < ALLN:
                            more = min(width, ALLN - width)
                            V.tensor_scalar_add(iota[:, width:width + more], iota[:, 0:more], float(width))\
                                .then_inc(s_wide_iota, 1)
                            width += more
                            wide_iotas += 1
                            dve.wait_ge(s_wide_iota, wide_iotas)
                        for b in range(EARLY_BATCHES):
                            early_messages(b, early_place)
                        wide(0, early_tiles=True)
                        dve.wait_ge(s_early_used, U + EARLY)
                    wide(layer)
                    for j in range(len(PARTS)):
                        final(layer, j)
                if layer == 0:
                    dve.wait_ge(s_deg_sum, 1)
                    V.tensor_copy(deg_sb[:, :], ps[0:8, DEG:DEG + BANK]).then_inc(s_deg, 1)
                elif layer == 1:
                    dve.wait_ge(s_x2, BLOCKS)

        @block.tensor
        def _(pe):
            T = nc.tensor

            def table_product(n, source, weight):
                b = n % BLOCKS
                if n >= 2:
                    pe.wait_ge(s_tab_sb, n - 1)
                T.matmul(ps[:, (n % 2) * BANK:(n % 2 + 1) * BANK], source[:, b * P:(b + 1) * P],
                         weight[:, :, :].rearrange("p r f -> p (r f)"), start=True, stop=True).then_inc(s_tab_mm, 1)

            def clear(j, rows=P):
                T.matmul(ps[0:rows, j * BANK:(j + 1) * BANK], zeros[:, 0:rows], zeros[:, :], start=True, stop=False,
                         skip_group_check=True)

            def close(j, rows=P):
                return T.matmul(ps[0:rows, j * BANK:(j + 1) * BANK], zeros[:, 0:rows], zeros[:, :], start=False,
                                stop=True, skip_group_check=True)

            def transposes(source, lo, hi, column):
                for b in range(lo, hi):
                    last = T.transpose(ps[:, column + (b - lo) * P:column + (b - lo + 1) * P], source(b), ident[:, :])
                return last

            def bases():
                pe.wait_ge(s_const, 10)
                pe.wait_ge(s_dstf, 1)
                T.matmul(ps[:, DEG:DEG + TILES], ones_row[:, :], dst_f[0:1, :], start=True, stop=True)\
                    .then_inc(s_base_mm, 1)

            def early_transposes(batch, first=False):
                pe.wait_ge(s_early_now, batch + 1)
                if not first:
                    pe.wait_ge(s_early_t, batch)
                for m in range(BATCH):
                    last = T.transpose(acc[:, BANKS - 1, m * P:(m + 1) * P], early_now[:, m, :], ident[:, :])
                last.then_inc(s_early_tr, 1)

            def early_products(batch, slot, first=False):
                pe.wait_ge(s_early_t, batch + 1)
                for m in range(BATCH):
                    if not first:
                        pe.wait_ge(s_early_msg, BATCH * batch + (m + 1 - BATCH))
                    T.matmul(acc[:, EARLY_BANKS + m, :], early_t[:, slot, m * P:(m + 1) * P],
                             wall[0][:, :, :].rearrange("p r f -> p (r f)"), start=True, stop=True)\
                        .then_inc(s_early_mm, 1)

            pe.sem_inc(s_used, U)
            pe.sem_inc(s_early_used, U)
            pe.wait_ge(s_ld_w1, 16)
            for n in range(BLOCKS):
                for part, (lo, hi) in enumerate(X_PARTS):
                    if n * P == lo:
                        pe.wait_ge(s_ld_x[part], 16)
                if n == FIRST_BATCH:
                    early_transposes(0, first=True)
                elif n == FIRST_BATCH + 1:
                    early_products(0, 0, first=True)
                table_product(n, x_t, wall[0])
                if n == 3:
                    bases()
            pe.wait_ge(s_ld_w, 128)
            pe.wait_ge(s_edges, 3)
            sorted_flag = pe.value_load(ok_i[0:1, 0:1], min_val=0, max_val=1)

            def registers(values, least, most):
                return nc.values_load_multi_w_load_instructions(
                    values, engines=[mybir.EngineType.PE], min_val=least, max_val=most,
                    skip_runtime_bounds_check_because="worked out from destinations, which are nodes")[1]

            def root_term(layer, source, j):
                clear(j)
                T.matmul(acc[:, j, 0:STRIDE], root[layer][:, :], source[:, j * STRIDE:(j + 1) * STRIDE],
                         start=False, stop=False, skip_group_check=True)

            def some_near(layer, i, lo, hi):
                half = HALVES[1][0] <= lo
                first = U * i + (U * FIRST_PASS[layer] + lo)
                cols = registers(col_i[0:1, bass.ds(first, hi - lo)], 0, BANKS * BANK - WIN)
                if layer == 0:
                    deg_cols = registers(deg_col_i[0:1, bass.ds(first, hi - lo)], DEG, 8 * BANK - WIN)
                pe.wait_ge(s_sel, 2 * i + (2 * BEFORE[layer] + half + 1))
                for k in range(lo, hi):
                    pe.wait_ge(s_msg[k], 16 * i + 16 * (BEFORE[layer] + 1))
                    last = T.matmul(ps[:, bass.ds(cols[k - lo], WIN)], msg[:, k, :], sel[:, k, :],
                                    start=False, stop=False, skip_group_check=True)
                    if layer == 0:
                        last = T.matmul(ps[0:8, bass.ds(deg_cols[k - lo], WIN)], deg_bank[:, k, :],
                                        hit_sel[:, k, :], start=False, stop=False, skip_group_check=True)
                    last.then_inc(s_used, 1)

            def half_near(layer, i, half):
                some_near(layer, i, *HALVES[half])

            def near_until(layer, at, to):
                if at < to and at % 2:
                    half_near(layer, at // 2 - FIRST_PASS[layer], 1)
                    at += 1
                if at // 2 < to // 2:
                    near(layer, at // 2, to // 2)
                if at < to and to % 2:
                    half_near(layer, to // 2 - FIRST_PASS[layer], 0)

            def near(layer, start, end):
                with pe.Fori(start - FIRST_PASS[layer], end - FIRST_PASS[layer]) as i:
                    for half in range(2):
                        half_near(layer, i, half)

            def early_sums(batch, slot):
                cols = registers(col_i[0:1, bass.ds(batch * BATCH, BATCH)], 0, BANKS * BANK - WIN)
                deg_cols = registers(deg_col_i[0:1, bass.ds(batch * BATCH, BATCH)], DEG, 8 * BANK - WIN)
                pe.wait_ge(s_early_sel, batch + 1)
                pe.wait_ge(s_early_msg, BATCH * batch + BATCH)
                for m in range(BATCH):
                    T.matmul(ps[0:8, bass.ds(deg_cols[m], WIN)], early_deg_bank[:, slot, m, :],
                             early_hit_sel[:, slot, m, :], start=False, stop=False, skip_group_check=True)
                    T.matmul(ps[:, bass.ds(cols[m], WIN)], early_msg[:, slot, m, :], early_sel[:, slot, m, :],
                             start=False, stop=False, skip_group_check=True).then_inc(s_early_used, 1)

            def wide(layer, early_tiles=False):
                with pe.Fori(0, EARLY_PASSES if early_tiles else ITERS - FIRST_PASS[layer]) as i:
                    for k in range(U):
                        if early_tiles:
                            message = early_msg[:, 0, k % 2, :]
                            pe.wait_ge(s_early_sel, 2 * U * i + 2 * (k + 1))
                            pe.wait_ge(s_early_hit, U * i + (k + 1))
                        else:
                            message = msg[:, k, :]
                            pe.wait_ge(s_msg[k], 16 * i + 16 * (BEFORE[layer] + 1))
                            pe.wait_ge(s_sel, U * i + (U * BEFORE[layer] + k + 1))
                            if layer == 0:
                                pe.wait_ge(s_hit, U * i + (k + 1))
                        for j in range(BANKS):
                            c = slice(j * STRIDE, (j + 1) * STRIDE)
                            last = T.matmul(acc[:, j, 0:STRIDE], message, wide_sel[:, k % 2, c],
                                            start=False, stop=False, skip_group_check=True)
                            if layer == 0:
                                last = T.matmul(ps[0:8, DEG:DEG + STRIDE], bank_col[:, j, :], wide_deg[:, k % 2, c],
                                                start=False, stop=False, skip_group_check=True)
                        last.then_inc(s_early_used if early_tiles else s_used, 1)

            def spread(banks):
                pe.wait_ge(s_deg, 1)
                for d in banks:
                    if d > 0:
                        pe.wait_ge(s_deg_b, d)
                    last = T.matmul(ps[:, DEG:DEG + STRIDE], row_sel[:, d, :], deg_sb[:, 0:STRIDE],
                                    start=True, stop=(d == 0), skip_group_check=True)
                    if d > 0:
                        last = T.matmul(ps[:, DEG:DEG + WIN], row_sel[:, d - 1, :], deg_sb[:, STRIDE:BANK],
                                        start=False, stop=True, skip_group_check=True)
                    last.then_inc(s_deg_mm, 1)

            def second_steps(j):
                lo, hi = READY[j], READY[j + 1]

                def transpose_x2():
                    pe.wait_ge(s_x2, hi)
                    transposes(lambda b: x2_nm[:, b, :], lo, hi, 0).then_inc(s_x2t_mm, 1)

                def third_table():
                    pe.wait_ge(s_x2t, j + 1)
                    for b in range(lo, hi):
                        last = T.matmul(ps[:, DEG + (b - lo) * P:DEG + (b - lo + 1) * P],
                                        x2_t[:, b * P:(b + 1) * P], wtop[:, :], start=True, stop=True)
                    last.then_inc(s_tab_mm, 1)
                    for n, d in enumerate(BEGUN[j]):
                        pe.wait_ge(s_dx, sum(map(len, BEGUN[:j])) + n + 1)
                        clear(d)
                        T.matmul(acc[:, d, 0:STRIDE], wbot[:, :], deg_x[:, d, :],
                                 start=False, stop=False, skip_group_check=True)
                return transpose_x2, third_table

            def final(layer, j):
                bank, _, end = PARTS[j]
                whole = end == STRIDE
                close(bank).then_inc(s_sum, 1)
                lo, hi = READY[j], READY[j + 1]
                if layer == 0:
                    if j == len(PARTS) - 1:
                        close(BANKS, 8).then_inc(s_deg_sum, 1)
                    if j > 0:
                        pe.wait_ge(s_h_act, j + 1)
                        pe.wait_ge(s_h_dve, bank)
                        for b in range(SECOND[j], SECOND[j + 1]):
                            table_product(BLOCKS + b, h_t, wall[1])
                    if bank > 1 and whole:
                        root_term(1, h_t, bank)
                elif layer == 1:
                    pe.wait_ge(s_z, j + 1)
                    pe.wait_ge(s_deg_b, BANKS)
                    pe.wait_ge(s_tab_sb, 2 * BLOCKS + j)
                    for b in range(lo, hi):
                        last = T.transpose(z_block(j, b), z_t[:, b * P:(b + 1) * P], ident[:, :])
                    last.then_inc(s_zn, 1)
                else:
                    pe.wait_ge(s_sig, bank + j + 1)
                    if j > 0:
                        pe.wait_ge(s_stat2, j)
                    transposes(lambda b: z_t[:, b * P:(b + 1) * P], lo, hi, DEG).then_inc(s_sn, 1)

            def sums(layer):
                with pe.If(sorted_flag == 1):
                    at = 0
                    if layer == 0:
                        clear(BANKS, 8)
                        for j in range(EARLY_BANKS):
                            root_term(0, x_t, j)
                        for b in range(1, AHEAD):
                            early_transposes(b)
                            if b > 1:
                                early_products(b - 1, (b - 1) % 2)
                                early_sums(b - 2, b % 2)
                        with pe.Fori(0, EARLY_LOOPS) as i:
                            for half in range(2):
                                half_near(0, i, half)
                                slot = (AHEAD + half) % 2
                                early_transposes(2 * i + (AHEAD + half))
                                early_products(2 * i + (AHEAD + half - 1), 1 - slot)
                                early_sums(2 * i + (AHEAD + half - 2), slot)
                        b = EARLY_BATCHES
                        early_products(b - 1, (b - 1) % 2)
                        early_sums(b - 2, b % 2)
                        pe.wait_ge(s_early_t, b)
                        for j in range(EARLY_BANKS + BATCH, BANKS):
                            root_term(0, x_t, j)
                        early_sums(b - 1, (b - 1) % 2)
                        root_term(0, x_t, EARLY_BANKS)
                        half_near(0, EARLY_LOOPS, 0)
                        half_near(0, EARLY_LOOPS, 1)
                        for j in range(EARLY_BANKS + 1, EARLY_BANKS + BATCH):
                            root_term(0, x_t, j)
                        at = 2 * (EARLY_END + 1)
                    for halves, what, arg in stops(layer):
                        near_until(layer, at, halves)
                        at = halves
                        final(layer, arg) if what == "final" else spread(arg)
                        if layer == 1 and what == "final":
                            transpose_x2, third_table = second_steps(arg)
                            if arg < LAST_HALF - 1:
                                near_until(1, at, at + 1)
                                transpose_x2()
                                near_until(1, at + 1, at + 2)
                                third_table()
                                at += 2
                            elif arg <= LAST_HALF:
                                lo, hi = HALVES[at % 2]
                                middle = (lo + hi) // 2
                                some_near(1, ITERS - 1, lo, middle)
                                transpose_x2()
                                some_near(1, ITERS - 1, middle, hi - 1)
                                third_table()
                                some_near(1, ITERS - 1, hi - 1, hi)
                                at += 1
                            else:
                                transpose_x2()
                                third_table()
                with pe.Else():
                    if layer == 0:
                        for b in range(1, EARLY_BATCHES):
                            early_transposes(b)
                            early_products(b, b % 2)
                        pe.wait_ge(s_early_msg, EARLY)
                        clear(BANKS, 8)
                        for j in range(BANKS):
                            root_term(0, x_t, j)
                        wide(0, early_tiles=True)
                    wide(layer)
                    for _, what, arg in stops(layer):
                        final(layer, arg) if what == "final" else spread(arg)
                        if layer == 1 and what == "final":
                            for step in second_steps(arg):
                                step()

            pe.wait_ge(s_tab_sb, FIRST_PIECE[1])
            sums(0)
            pe.wait_ge(s_tab_sb, FIRST_PIECE[2])
            for j in range(2):
                root_term(1, h_t, j)
            sums(1)
            sums(2)


def edges_by_tile(a):
    return np.ascontiguousarray(np.pad(np.asarray(a), (0, TILES * P - N_EDGES), mode="edge").reshape(TILES, P).T)


def kernel(x, src, dst, edge_type_4, edge_weight, L0_gnn_W1, L0_gnn_root1, L0_gnn_b1, L0_gnn_W2, L0_gnn_root2,
           L0_gnn_b2, L1_gnn_W, L1_gnn_b):
    import concourse.bacc as bacc
    from concourse.bass_utils import run_bass_kernel_spmd

    laid = {
        "x": np.pad(np.asarray(x), ((0, NP - N_NODES), (0, 0))).T,
        "x_rows": x,
        "src": edges_by_tile(src), "dst": edges_by_tile(dst),
        "types": edges_by_tile(edge_type_4), "weights": edges_by_tile(edge_weight),
        "w1": L0_gnn_W1, "root1": L0_gnn_root1, "b1": L0_gnn_b1,
        "w2": L0_gnn_W2, "root2": L0_gnn_root2, "b2": L0_gnn_b2, "w3": L1_gnn_W, "b3": L1_gnn_b,
    }
    nc = bacc.Bacc("TRN2", target_bir_lowering=False, num_devices=1)
    arrays, args = {}, []
    for name, a in laid.items():
        a = np.ascontiguousarray(a)
        arrays[f"in_{name}"] = a
        args.append(nc.dram_tensor(f"in_{name}", a.shape, mybir.dt.from_np(a.dtype), kind="ExternalInput").ap())
    args.append(nc.dram_tensor("out_y", (N_NODES, FEAT), mybir.dt.float32, kind="ExternalOutput").ap())
    build(nc, *args)
    r = run_bass_kernel_spmd(nc, [arrays], core_ids=[0])
    return r.results[0]["out_y"]
```
